# Optimizing a Trainium2 kernel written in Bass

```python
import numpy as np
import jax
import jax.numpy as jnp

def _softmax(x, axis=-1):
    return jax.nn.softmax(x, axis=axis)

def _gelu(x):
    return jax.nn.gelu(x, approximate=True)

def _silu(x):
    return jax.nn.silu(x)

def _sigmoid(x):
    return jax.nn.sigmoid(x)

def _layernorm(x, axis=-1, eps=1e-05):
    m = jnp.mean(x, axis=axis, keepdims=True)
    v = jnp.var(x, axis=axis, keepdims=True)
    return (x - m) / jnp.sqrt(v + eps)

def _scatter_add(tgt, idx, src, axis=0):
    return tgt.at[idx].add(src)

def _segment_sum(src, seg, n):
    return jax.ops.segment_sum(src, seg, n)
kernel_name = 'mk_prb_d2_jaxref_r4_33134e'

def setup_inputs(seed: int=0):
    np.random.seed(seed)
    _w = jnp.asarray

    def _L0_attn_setup():
        import jax, jax.numpy as jnp
        import numpy as np
        D_MODEL = 512
        NUM_HEADS = 16
        DILATION = 2
        SEG = 128
        HEAD_DIM = D_MODEL // NUM_HEADS

        def _dilated_attention(x):
            B, N, D = x.shape
            w, r, H, hd = (SEG, DILATION, NUM_HEADS, HEAD_DIM)
            pad = -N % w
            x = jnp.pad(x, ((0, 0), (0, pad), (0, 0)))
            Np = N + pad
            nseg = Np // w
            s = w // r
            xs = x.reshape(B, nseg, w, H, hd).transpose(0, 1, 3, 2, 4)
            offsets = jnp.arange(H) % r
            idx = offsets[:, None] + jnp.arange(s)[None, :] * r
            g = jnp.take_along_axis(xs, idx[None, None, :, :, None], axis=3)
            scale = jnp.asarray(hd, x.dtype) ** (-0.5)
            scores = jnp.einsum('bnhqd,bnhkd->bnhqk', g, g) * scale
            attn = jax.nn.softmax(scores, axis=-1)
            out = jnp.einsum('bnhqk,bnhkd->bnhqd', attn, g)
            out_full = jnp.zeros((B, nseg, H, w, hd), dtype=x.dtype)
            out_full = out_full.at[:, :, jnp.arange(H)[:, None], idx, :].set(out)
            out_full = out_full.transpose(0, 1, 3, 2, 4).reshape(B, Np, D)
            return out_full[:, :N, :]
        key = jax.random.key(seed)
        x = jax.random.normal(key, (4, 2048, D_MODEL), dtype=jnp.float32)
        return {'x': x}
    _L0_attn_in = _L0_attn_setup()

    def _L0_ffn_setup():
        import jax, jax.numpy as jnp
        import numpy as np
        QMAX = 127.0
        QMIN = -128.0
        key = jax.random.key(seed)
        k1, k2, k3 = jax.random.split(key, 3)
        B, N, D, O = (4, 1024, 512, 512)
        x = jax.random.normal(k1, (B, N, D), dtype=jnp.float32)
        weight = jax.random.normal(k2, (O, D), dtype=jnp.float32)
        bias = jax.random.normal(k3, (O,), dtype=jnp.float32)
        return {'x': x, 'weight': weight, 'bias': bias}
    _L0_ffn_in = _L0_ffn_setup()

    def _L1_attn_setup():
        import jax, jax.numpy as jnp
        import numpy as np
        from jax import lax
        B, L, H = (2, 1024, 512)
        NH = 16
        DK = H // NH
        C = 64
        EPS = 1e-05
        N_LAYER = 24

        def _gla_chunk(q, k, v, gf):
            b, Ls, dk = q.shape
            dv = v.shape[-1]
            n = Ls // C
            qc = q.reshape(b, n, C, dk).transpose(1, 0, 2, 3)
            kc = k.reshape(b, n, C, dk).transpose(1, 0, 2, 3)
            vc = v.reshape(b, n, C, dv).transpose(1, 0, 2, 3)
            gc = gf.reshape(b, n, C, dk).transpose(1, 0, 2, 3)
            Bc = jnp.cumsum(gc, axis=2)
            tril = jnp.tril(jnp.ones((C, C), bool))

            def step(S, inp):
                qh, kh, vh, Bh = inp
                Blast = Bh[:, -1, :]
                D = Bh[:, :, None, :] - Bh[:, None, :, :]
                A = jnp.einsum('bid,bjd,bijd->bij', qh, kh, jnp.exp(D))
                A = jnp.where(tril, A, 0.0)
                o_intra = jnp.einsum('bij,bjv->biv', A, vh)
                o_inter = jnp.einsum('bid,bdv->biv', qh * jnp.exp(Bh), S)
                kd = kh * jnp.exp(Blast[:, None, :] - Bh)
                S_new = S * jnp.exp(Blast)[..., None] + jnp.einsum('bjd,bjv->bdv', kd, vh)
                return (S_new, o_intra + o_inter)
            S0 = jnp.zeros((b, dk, dv), q.dtype)
            _, o = lax.scan(step, S0, (qc, kc, vc, Bc))
            return o.transpose(1, 0, 2, 3).reshape(b, Ls, dv)
        key = jax.random.key(seed)
        ks = jax.random.split(key, 7)
        std = 0.02
        return {'hidden_states': jax.random.normal(ks[0], (B, L, H), jnp.float32), 'Wq': jax.random.normal(ks[1], (DK, H), jnp.float32) * std, 'Wk': jax.random.normal(ks[2], (DK, H), jnp.float32) * std, 'Wog': jax.random.normal(ks[3], (H, H), jnp.float32) * std, 'Wig': jax.random.normal(ks[4], (H, H), jnp.float32) * std, 'Wo': jax.random.normal(ks[5], (H, H), jnp.float32) * (std / np.sqrt(2 * N_LAYER)), 'g_norm_w': jnp.ones((H,), jnp.float32)}
    _L1_attn_in = _L1_attn_setup()

    def _L1_ffn_setup():
        import jax, jax.numpy as jnp
        import numpy as np
        B, T = (1, 128)
        DIM = 512
        MOE_INTER = 352
        N_EXPERTS = 64
        TOPK = 6
        N_SHARED = 2
        SHARED_INTER = N_SHARED * MOE_INTER
        CAPACITY = 128
        ROUTE_SCALE = 1.0
        key = jax.random.key(seed)
        ks = jax.random.split(key, 8)

        def w(k, shape, fan_in):
            return jax.random.normal(k, shape, jnp.float32) * fan_in ** (-0.5)
        return {'x': jax.random.normal(ks[0], (B, T, DIM), jnp.float32), 'gate_w': w(ks[1], (N_EXPERTS, DIM), DIM), 'w1': w(ks[2], (N_EXPERTS, MOE_INTER, DIM), DIM), 'w2': w(ks[3], (N_EXPERTS, DIM, MOE_INTER), MOE_INTER), 'w3': w(ks[4], (N_EXPERTS, MOE_INTER, DIM), DIM), 'sw1': w(ks[5], (SHARED_INTER, DIM), DIM), 'sw2': w(ks[6], (DIM, SHARED_INTER), SHARED_INTER), 'sw3': w(ks[7], (SHARED_INTER, DIM), DIM)}
    _L1_ffn_in = _L1_ffn_setup()
    _d = {'L0_attn_x': _L0_attn_in['x'], 'L0_ffn_weight': _L0_ffn_in['weight'], 'L0_ffn_bias': _L0_ffn_in['bias'], 'L1_attn_Wq': _L1_attn_in['Wq'], 'L1_attn_Wk': _L1_attn_in['Wk'], 'L1_attn_Wog': _L1_attn_in['Wog'], 'L1_attn_Wig': _L1_attn_in['Wig'], 'L1_attn_Wo': _L1_attn_in['Wo'], 'L1_attn_g_norm_w': _L1_attn_in['g_norm_w'], 'L1_ffn_gate_w': _L1_ffn_in['gate_w'], 'L1_ffn_w1': _L1_ffn_in['w1'], 'L1_ffn_w2': _L1_ffn_in['w2'], 'L1_ffn_w3': _L1_ffn_in['w3'], 'L1_ffn_sw1': _L1_ffn_in['sw1'], 'L1_ffn_sw2': _L1_ffn_in['sw2'], 'L1_ffn_sw3': _L1_ffn_in['sw3']}
    _x0 = _d['L0_attn_x']
    _d['L0_attn_x'] = jax.random.normal(jax.random.fold_in(jax.random.key(seed), 1), (1, 2048, 512), dtype=_x0.dtype)
    del _x0
    return _d

def reference(L0_attn_x, L0_ffn_weight, L0_ffn_bias, L1_attn_Wq, L1_attn_Wk, L1_attn_Wog, L1_attn_Wig, L1_attn_Wo, L1_attn_g_norm_w, L1_ffn_gate_w, L1_ffn_w1, L1_ffn_w2, L1_ffn_w3, L1_ffn_sw1, L1_ffn_sw2, L1_ffn_sw3):

    def _L0_attn_ref(x):
        import jax, jax.numpy as jnp
        import numpy as np
        D_MODEL = 512
        NUM_HEADS = 16
        DILATION = 2
        SEG = 128
        HEAD_DIM = D_MODEL // NUM_HEADS

        def _dilated_attention(x):
            B, N, D = x.shape
            w, r, H, hd = (SEG, DILATION, NUM_HEADS, HEAD_DIM)
            pad = -N % w
            x = jnp.pad(x, ((0, 0), (0, pad), (0, 0)))
            Np = N + pad
            nseg = Np // w
            s = w // r
            xs = x.reshape(B, nseg, w, H, hd).transpose(0, 1, 3, 2, 4)
            offsets = jnp.arange(H) % r
            idx = offsets[:, None] + jnp.arange(s)[None, :] * r
            g = jnp.take_along_axis(xs, idx[None, None, :, :, None], axis=3)
            scale = jnp.asarray(hd, x.dtype) ** (-0.5)
            scores = jnp.einsum('bnhqd,bnhkd->bnhqk', g, g) * scale
            attn = jax.nn.softmax(scores, axis=-1)
            out = jnp.einsum('bnhqk,bnhkd->bnhqd', attn, g)
            out_full = jnp.zeros((B, nseg, H, w, hd), dtype=x.dtype)
            out_full = out_full.at[:, :, jnp.arange(H)[:, None], idx, :].set(out)
            out_full = out_full.transpose(0, 1, 3, 2, 4).reshape(B, Np, D)
            return out_full[:, :N, :]
        return _dilated_attention(x)

    def _L0_ffn_ref(x, weight, bias):
        import jax, jax.numpy as jnp
        import numpy as np
        QMAX = 127.0
        QMIN = -128.0
        w_max = jnp.clip(jnp.max(jnp.abs(weight), axis=1, keepdims=True), 1e-08, None)
        w_scale = w_max / QMAX
        w_q = jnp.clip(jnp.round(weight / w_scale), QMIN, QMAX).astype(jnp.int8)
        w_scale = w_scale.squeeze(1).astype(jnp.float32)
        x_max = jnp.max(jnp.abs(x), axis=2, keepdims=True)
        x_scale = jnp.maximum(x_max / QMAX, 1e-12)
        x_q = jnp.clip(jnp.round(x / x_scale), QMIN, QMAX).astype(jnp.int8)
        acc = jnp.einsum('bnd,od->bno', x_q.astype(jnp.int32), w_q.astype(jnp.int32))
        y = acc.astype(jnp.float32) * x_scale.astype(jnp.float32) * w_scale[None, None, :]
        y = y + bias
        return y.astype(x.dtype)

    def _L1_attn_ref(hidden_states, Wq, Wk, Wog, Wig, Wo, g_norm_w):
        import jax, jax.numpy as jnp
        import numpy as np
        from jax import lax
        B, L, H = (2, 1024, 512)
        NH = 16
        DK = H // NH
        C = 64
        EPS = 1e-05
        N_LAYER = 24

        def _gla_chunk(q, k, v, gf):
            b, Ls, dk = q.shape
            dv = v.shape[-1]
            n = Ls // C
            qc = q.reshape(b, n, C, dk).transpose(1, 0, 2, 3)
            kc = k.reshape(b, n, C, dk).transpose(1, 0, 2, 3)
            vc = v.reshape(b, n, C, dv).transpose(1, 0, 2, 3)
            gc = gf.reshape(b, n, C, dk).transpose(1, 0, 2, 3)
            Bc = jnp.cumsum(gc, axis=2)
            tril = jnp.tril(jnp.ones((C, C), bool))

            def step(S, inp):
                qh, kh, vh, Bh = inp
                Blast = Bh[:, -1, :]
                D = Bh[:, :, None, :] - Bh[:, None, :, :]
                A = jnp.einsum('bid,bjd,bijd->bij', qh, kh, jnp.exp(D))
                A = jnp.where(tril, A, 0.0)
                o_intra = jnp.einsum('bij,bjv->biv', A, vh)
                o_inter = jnp.einsum('bid,bdv->biv', qh * jnp.exp(Bh), S)
                kd = kh * jnp.exp(Blast[:, None, :] - Bh)
                S_new = S * jnp.exp(Blast)[..., None] + jnp.einsum('bjd,bjv->bdv', kd, vh)
                return (S_new, o_intra + o_inter)
            S0 = jnp.zeros((b, dk, dv), q.dtype)
            _, o = lax.scan(step, S0, (qc, kc, vc, Bc))
            return o.transpose(1, 0, 2, 3).reshape(b, Ls, dv)
        x = hidden_states
        q = jax.nn.softmax(x @ Wq.T, axis=-1)
        k = jax.nn.sigmoid(x @ Wk.T)
        v = x
        gf = jax.nn.log_sigmoid(-k)
        o = _gla_chunk(q, k, v, gf)
        go = o @ Wog.T + x @ Wig.T
        on = o * lax.rsqrt(jnp.mean(o * o, axis=-1, keepdims=True) + EPS) * g_norm_w
        o = on * (go * jax.nn.sigmoid(go))
        return o @ Wo.T

    def _L1_ffn_ref(x, gate_w, w1, w2, w3, sw1, sw2, sw3):
        import jax, jax.numpy as jnp
        import numpy as np
        B, T = (1, 128)
        DIM = 512
        MOE_INTER = 352
        N_EXPERTS = 64
        TOPK = 6
        N_SHARED = 2
        SHARED_INTER = N_SHARED * MOE_INTER
        CAPACITY = 128
        ROUTE_SCALE = 1.0
        Bb, Tt, D = x.shape
        xf = x.reshape(-1, D)
        N = xf.shape[0]
        logits = xf @ gate_w.T
        scores = jax.nn.softmax(logits, axis=-1)
        gate_vals, idx = jax.lax.top_k(scores, TOPK)
        gate_vals = gate_vals * ROUTE_SCALE
        E = gate_w.shape[0]
        fe = idx.reshape(-1)
        ft = jnp.repeat(jnp.arange(N), TOPK)
        onehot = (fe[:, None] == jnp.arange(E)[None, :]).astype(jnp.int32)
        pos = jnp.take_along_axis(jnp.cumsum(onehot, axis=0) - 1, fe[:, None], axis=1)[:, 0]
        keep = pos < CAPACITY
        buf = jnp.full((E, CAPACITY), N, dtype=jnp.int32)
        buf = buf.at[fe, pos].set(ft.astype(jnp.int32), mode='drop')
        xpad = jnp.concatenate([xf, jnp.zeros((1, D), xf.dtype)], axis=0)
        xe = xpad[buf]
        h = jax.nn.silu(jnp.einsum('ecd,eid->eci', xe, w1)) * jnp.einsum('ecd,eid->eci', xe, w3)
        ye = jnp.einsum('eci,edi->ecd', h, w2)
        pc = jnp.minimum(pos, CAPACITY - 1)
        op = ye[fe, pc] * keep[:, None].astype(ye.dtype)
        routed = (op * gate_vals.reshape(-1)[:, None]).reshape(N, TOPK, D).sum(axis=1)
        z = jax.nn.silu(xf @ sw1.T) * (xf @ sw3.T) @ sw2.T
        return (routed + z).reshape(Bb, Tt, D)
    x = L0_attn_x
    xn = _layernorm(x, axis=-1)
    x = x + _L0_attn_ref(xn) + _L0_ffn_ref(xn, L0_ffn_weight, L0_ffn_bias)
    xn = _layernorm(x, axis=-1)
    x = x + _L1_attn_ref(xn, L1_attn_Wq, L1_attn_Wk, L1_attn_Wog, L1_attn_Wig, L1_attn_Wo, L1_attn_g_norm_w) + _L1_ffn_ref(xn, L1_ffn_gate_w, L1_ffn_w1, L1_ffn_w2, L1_ffn_w3, L1_ffn_sw1, L1_ffn_sw2, L1_ffn_sw3)
    return x

_drawn_inputs = setup_inputs


def setup_inputs(seed=0):
    import zlib

    import numpy as np

    out = dict(_drawn_inputs(seed))
    spreads = {'L1_attn_g_norm_w': (1.0, 0.6)}
    factors = {'L1_attn_Wq': 64.0,
     'L1_attn_Wk': 64.0,
     'L1_attn_Wog': 64.0,
     'L1_attn_Wig': 64.0,
     'L1_attn_Wo': 48.882,
     'L1_ffn_gate_w': 8.0,
     'L1_ffn_w1': 8.0,
     'L1_ffn_w2': 8.0,
     'L1_ffn_w3': 8.0,
     'L1_ffn_sw1': 8.0,
     'L1_ffn_sw2': 8.0,
     'L1_ffn_sw3': 8.0}
    for name, (base, spread) in spreads.items():
        noise = np.random.default_rng([zlib.crc32(name.encode()), seed]).standard_normal(out[name].shape)
        drawn = base * np.exp(spread * noise) if base else spread * noise
        out[name] = jnp.asarray(drawn.astype(out[name].dtype))
    for name, factor in factors.items():
        out[name] = (out[name] * factor).astype(out[name].dtype)
    return out
```

```python
import concourse.bass as bass
from concourse import mybir
from contextlib import ExitStack


class At:

    def __init__(self, i, off):
        self.i, self.off, self.b = i, off, off % 2

    def n(self, add=0):
        return self.i * 2 + (self.off + add)

    def dma(self, back=0):
        return self.i * 16 + 16 * (self.off // 2 + 1 - back)

    def dma2(self):
        return self.i * 32 + 32 * (self.off // 2 + 1)

    def past(self, k):
        return not isinstance(self.i, int) or self.off >= k

    def plus(self, k):
        return At(self.i, self.off + k)


class Turn:

    def __init__(self, at, count):
        static = isinstance(at.i, int)
        self.prev = at.plus(-1) if at.off >= 1 else None
        self.cur = at if not static or at.off < count else None
        self.next = at.plus(1) if not static or at.off + 1 < count else None
        self.after = at.plus(2) if not static or at.off + 2 < count else None


def turns(engine, count, turn, tail):
    for k in range(3):
        turn(Turn(At(0, k), count))
    with engine.Fori(0, (count - 3 - tail) // 2) as i:
        turn(Turn(At(i, 3), count))
        turn(Turn(At(i, 4), count))
    for k in range(count - tail, count + 1):
        turn(Turn(At(0, k), count))


def two_layers(nc, x, w_ffn, b_ffn, w_rqk, w_og, w_ig, w_o, g_norm, w_sh13, w_sh2, w13, w2a, w2b, out,
               xn_rows, ye_rows):
    f32, bf16, u32 = mybir.dt.float32, mybir.dt.bfloat16, mybir.dt.uint32
    ALU, ACT, AX = mybir.AluOpType, mybir.ActivationFunctionType, mybir.AxisListType

    P = 128
    N, D = x.shape
    NT = N // P
    DC = D // P
    H, HD = 16, 32
    HP = H // 2
    SEGQ = P // 2
    NE, TOPK, CAP = w13.shape[0], 6, 128
    I2 = w13.shape[3]
    IE = I2 // 2
    IA, IB = 2 * P, IE - 2 * P
    SI = w_sh13.shape[2] // 2
    SQ = SI // 2
    SC = -(-SI // P)
    SR = SI - (SC - 1) * P
    DK = 32
    ATT_SCALE = float(HD) ** -0.5
    EPS = 1e-5
    MAGIC = 12582912.0
    QMAX = 127.0

    x_tiles = x.rearrange("(t j r) d -> t r j d", r=2, j=SEGQ)
    out_tiles = out.rearrange("(t j r) d -> t r j d", r=2, j=SEGQ)
    xn_tiles = xn_rows.rearrange("(t p) d -> t p d", p=P)
    ye_tiles = ye_rows.rearrange("(e p) d -> e p d", p=CAP)

    ctx = ExitStack()
    with ctx:
        def sb(name, shape, dt=f32):
            return ctx.enter_context(nc.sbuf_tensor(name, shape, dt))

        def pb(name, shape, dt=f32):
            return ctx.enter_context(nc.psum_tensor(name, shape, dt))

        def sem(name):
            return ctx.enter_context(nc.semaphore(name))

        ident = sb("ident", [P, P])
        ident_bf = sb("ident_bf", [P, P], bf16)
        ones_mat = sb("ones_mat", [P, P])
        ones_bf = sb("ones_bf", [P, P], bf16)
        slot_row = sb("slot_row", [P, P])
        slot_row_bf = sb("slot_row_bf", [P, P], bf16)
        token_row = sb("token_row", [P, P])
        part_col = sb("part_col", [P, 1])
        token_col = sb("token_col", [P, 1])
        chunk_row = sb("chunk_row", [P, P])
        chunk_col = sb("chunk_col", [P, 1])
        tmp_col = sb("tmp_col", [P, 4])
        same_chunk = sb("same_chunk", [P, P])
        causal = sb("causal", [P, P])
        first_half = sb("first_half", [P, P])
        from_mid = sb("from_mid", [P, P])
        to_last = sb("to_last", [P, P])
        before_bf = sb("before_bf", [P, P], bf16)
        head_rows = sb("head_rows", [P, 2 * DC, 2])
        head_want = sb("head_want", [P, 2 * DC, 2])
        chunk_of = sb("chunk_of", [P, 2])
        token_parts = sb("token_parts", [P, NT, 2], bf16)
        bias_bc = sb("bias_bc", [P, D])
        wscale_bc = sb("wscale_bc", [P, D])
        gnorm = sb("gnorm", [P, DC])
        wqT = sb("wqT", [P, DC, D], bf16)
        wrqk = sb("wrqk", [P, DC, P])
        big_w = sb("big_w", [P, DC * 2 * SI + SC * D])
        wsh13 = big_w[:, 0:DC * 2 * SI].rearrange("p (c i) -> p c i", c=DC)
        wsh2 = big_w[:, DC * 2 * SI:].rearrange("p (c d) -> p c d", c=SC)
        w_att = big_w[:, 0:3 * DC * D].rearrange("p (m c d) -> p m c d", m=3, c=DC)
        w13_sb = sb("w13_sb", [P, 2, DC, I2])
        w2_sb = sb("w2_sb", [P, 2, 3, D])

        acc = sb("acc", [P, NT, D])
        qk_logits = sb("qk_logits", [P, NT, 2 * DK])
        posm = sb("posm", [P, NE, NT], bf16)
        gates = sb("gates", [P, NT, TOPK])
        rows_of = sb("rows_of", [P, NT, TOPK], u32)

        work = sb("work", [P, 12800])
        used = [0]

        def wk(*shape):
            size = 1
            for s in shape:
                size *= s
            v = work[:, used[0]:used[0] + size]
            used[0] += size
            assert used[0] <= 12800
            if len(shape) == 1:
                return v
            names = "abcd"[:len(shape)]
            return v.rearrange(f"p ({' '.join(names)}) -> p {' '.join(names)}",
                               **{k: s for k, s in zip(names[:-1], shape[:-1])})

        wn = acc[:, 0:DC, :]
        wdiag = acc[:, DC, :].rearrange("p (c k) -> p c k", c=DC)
        wq = sb("wq", [P, DC, D], bf16)
        wcols = sb("wcols", [P, 3, DC])
        xin = wk(2, D)
        xn = wk(2, D)
        x_bias = wk(2, D)
        xnT = wk(DC, P)
        xn_heads = wk(2 * DC, 2, SEGQ)
        dist = wk(HP, SEGQ)
        eT = wk(HP, P)
        y = wk(D)
        att = wk(HP, 2, HD)
        x1 = wk(2, D)
        xn2 = wk(2, D)
        xn2T = wk(DC, P)
        hs = wk(SI)
        hsT = wk(SC, P)
        probs = sb("probs", [P, HP, P])
        xq_f = wk(D)
        xq = sb("xq", [P, D], bf16)
        xqT = sb("xqT", [P, DC, P], bf16)
        stats = sb("stats", [P, 2, 6])
        mv = sb("mv", [P, 2, 2])
        rstd = sb("rstd", [P, 2, 1])
        epow = sb("epow", [P, 1])
        xmax = sb("xmax", [P, 1])
        xscale = sb("xscale", [P, 2, 1])
        xinv = sb("xinv", [P, 1])
        smax = sb("smax", [P, HP])
        esum = sb("esum", [P, HP])
        einv = sb("einv", [P, HP])
        gmax = sb("gmax", [P, 1])
        glog = sb("glog", [P, NE])
        gexp = sb("gexp", [P, NE])
        gsum = sb("gsum", [P, 1])
        ginv = sb("ginv", [P, 1])
        score = sb("score", [P, NE])
        top_v = sb("top_v", [P, 8])
        top_i = sb("top_i", [P, 8], u32)
        top_f = sb("top_f", [P, 8])
        chosen = sb("chosen", [P, TOPK, NE])
        mask_bf = sb("mask_bf", [P, NE], bf16)
        msum_bf = sb("msum_bf", [P, NE], bf16)
        chosen_pos = sb("chosen_pos", [P, TOPK, NE])
        pos_k = sb("pos_k", [P, TOPK])
        pos_c = sb("pos_c", [P, TOPK])
        keep = sb("keep", [P, TOPK])
        posm_f = sb("posm_f", [P, NE])
        used[0] = 0
        hot = sb("hot", [P, NT, CAP], bf16)
        xe = wk(2, D)
        xeT = wk(2, DC, P)
        hsil = wk(IE)
        he = wk(2, IE)
        heT = wk(3, P)
        ye = wk(2, D)
        row_f = sb("row_f", [P, 1])
        row_i = sb("row_i", [P, 2, 1], u32)
        used[0] = 0
        v_t = wk(2, D)
        vT = wk(DC, P)
        o_sb = wk(D)
        oT = wk(DC, P)
        sil = wk(D)
        og = wk(D)
        ogT = wk(DC, P)
        gat = wk(TOPK, D)
        racc = wk(2, D)
        res = wk(2, D)
        state = wk(2, D)
        attT = wk(P)
        att_l = wk(4, P)
        softq = wk(DK)
        klog = wk(DK)
        kexp = wk(DK)
        qk = wk(2, DK)
        kgate = wk(DK)
        gfn = wk(DK)
        ex = wk(4, DK)
        exm = wk(DK)
        q_mid, k_mid = wk(DK), wk(DK)
        decay = wk(2, DK)
        qk_e = wk(2, DK)
        qk_c = wk(2, 2, DK)
        qmaxn, qsum, qinv, osq, orstd = wk(1), wk(1), wk(1), wk(1), wk(1)
        row_k = sb("row_k", [P, 2, TOPK], u32)

        bank = [pb(f"bank{i}", [P, 512]) for i in range(8)]

        def split4(b):
            return b[:, :].rearrange("p (c k) -> p c k", c=4)

        s_wn, s_wst, s_c0 = sem("s_wn"), sem("s_wst"), sem("s_c0")
        s_iota, s_const, s_set = sem("s_iota"), sem("s_const"), sem("s_set")
        s_wq, s_wqT, s_wqe, s_wsb, s_zero = sem("s_wq"), sem("s_wqT"), sem("s_wqe"), sem("s_wsb"), sem("s_zero")
        s_wsh = sem("s_wsh")
        s_dve_apart, s_pool_apart = sem("s_dve_apart"), sem("s_pool_apart")
        x_in = [sem("x_in0"), sem("x_in1")]
        names = ("stat1 var1 rstd1 ln_steps xn_done xq_done xb_done xnT_ps xqT_ps xnT_sb xqT_sb xnh_done s_ps "
                 "smax_done dist_done exp_done esum_done f_ps eT_ps0 eT_ps1 eT_sb att_ps sum_steps x1_done stat2 var2 "
                 "rstd2 xn2_done xn2T_ps xn2T_sb lg_ps lg_sb gmax_done gexp_done rt_steps mask_done pos_ps "
                 "slot_steps wa_ps wb_ps wc_ps wd_ps silA silB hA_done hB_done hT_ps hT_sb z_ps acc_done")
        a = {k: sem("a_" + k) for k in names.split()}
        xn_out = [sem("xn_out0"), sem("xn_out1")]
        w13_in = [sem("w13_in0"), sem("w13_in1")]
        w2_in = [sem("w2_in0"), sem("w2_in1")]
        w2r_in = [sem("w2r_in0"), sem("w2r_in1")]
        xe_in = [sem("xe_in0"), sem("xe_in1")]
        ye_out = [sem("ye_out0"), sem("ye_out1")]
        names = ("hot_done slot_ps row_done xeT_ps xeT_sb h1_ps h3_ps sil_done h_done hT_ps hT_sb y_ps y_sb")
        e_ = {k: sem("b_" + k) for k in names.split()}
        w_att_in = sem("w_att_in")
        v_in = [sem("v_in0"), sem("v_in1")]
        gat_in = [sem(f"gat_in{k}") for k in range(TOPK)]
        res_out = [sem("res_out0"), sem("res_out1")]
        names = ("qmax eq_done kexp_done qk_steps qk_done kgate_done gf_done cum_ps ex_done exm_done "
                 "nat_done gT_ps gT_sb vT_ps vT_sb at_ps at_sb ds_ps qk_e s_mid s_next wig_ps o_ps o_sb sq_done "
                 "ms_done rstd oT_ps oT_sb go_ps sil_done og_done ogT_ps ogT_sb out_ps res_done gat_used row_k")
        c = {k: sem("c_" + k) for k in names.split()}

        block = ctx.enter_context(nc.Block())

        @block.sync
        def _(sp):
            def load_x(t):
                for r in range(2):
                    sp.dma_start(xin[r * SEGQ:(r + 1) * SEGQ, t.b, :],
                                 x_tiles[bass.ds(t.n(), 1), r, :, :].rearrange("o j d -> (o j) d")
                                 ).then_inc(x_in[t.b], 16)

            load_x(At(0, 0))
            sp.dma_start(wn, w_ffn.rearrange("(c p) d -> p c d", p=P)).then_inc(s_wn, 16)
            sp.dma_start(bias_bc[:, :], b_ffn.partition_broadcast(P)).then_inc(s_c0, 16)
            sp.dma_start(gnorm[:, :], g_norm).then_inc(s_c0, 16)
            sp.dma_start(wrqk[:, :, :], w_rqk).then_inc(s_c0, 16)
            sp.dma_start(wsh13, w_sh13).then_inc(s_wsh, 16)
            sp.dma_start(wsh2[:, 0:SC - 1, :],
                         w_sh2[0:(SC - 1) * P, :].rearrange("(c p) d -> p c d", p=P)).then_inc(s_wsh, 16)
            sp.dma_start(wsh2[0:SR, SC - 1, :], w_sh2[(SC - 1) * P:SI, :]).then_inc(s_wsh, 16)

            load_x(At(0, 1))

            def load_w13(e):
                sp.dma_start(w13_sb[:, e.b, :, :],
                             w13[bass.ds(e.n(), 1), :, :, :].rearrange("o p c i -> (o p) c i")
                             ).then_inc(w13_in[e.b], 16)

            def load_w2(e):
                sp.dma_start(w2_sb[:, e.b, 0:2, :],
                             w2a[bass.ds(e.n(), 1), :, :, :].rearrange("o p c d -> (o p) c d")
                             ).then_inc(w2_in[e.b], 16)
                sp.dma_start(w2_sb[0:IB, e.b, 2, :],
                             w2b[bass.ds(e.n(), 1), :, :].rearrange("o p d -> (o p) d")
                             ).then_inc(w2r_in[e.b], 16)

            for e in range(2):
                load_w13(At(0, e))
                load_w2(At(0, e))

            def phase_a(t):
                sp.wait_ge(a["xn2_done"], t.n(1))
                sp.dma_start(xn_tiles[bass.ds(t.n(), 1), :, :].rearrange("o p d -> (o p) d"),
                             xn2[:, t.b, :]).then_inc(xn_out[t.b], 16)

            for t in (0,):
                sp.wait_ge(a["xb_done"], 1)
                sp.wait_ge(a["xn_done"], 1)
                load_x(At(0, 2))
                phase_a(At(0, 0))
            with sp.Fori(0, (NT - 4) // 2) as i:
                for off in (1, 2):
                    t = At(i, off)
                    sp.wait_ge(a["xb_done"], t.n(1))
                    sp.wait_ge(a["xn_done"], t.n(1))
                    load_x(t.plus(2))
                    phase_a(t)
            sp.wait_ge(a["xb_done"], NT - 2)
            sp.wait_ge(a["xn_done"], NT - 2)
            load_x(At(0, NT - 1))
            for t in (NT - 3, NT - 2, NT - 1):
                phase_a(At(0, t))

            def phase_b(e):
                sp.wait_ge(e_["y_sb"], e.n(1))
                sp.dma_start(ye_tiles[bass.ds(e.n(), 1), :, :].rearrange("o p d -> (o p) d"),
                             ye[:, e.b, :]).then_inc(ye_out[e.b], 16)

            def ahead(e, w13_too=True):
                sp.wait_ge(e_["h3_ps"], e.n(1))
                load_w13(e.plus(2))

            def ahead2(e):
                sp.wait_ge(e_["y_ps"], e.n(1))
                load_w2(e.plus(2))

            ahead(At(0, 0))
            with sp.Fori(0, (NE - 4) // 2) as i:
                for off in (1, 2):
                    e = At(i, off)
                    ahead(e)
                    ahead2(e.plus(-1))
                    phase_b(e.plus(-1))
            ahead(At(0, NE - 3))
            for e in (NE - 4, NE - 3):
                ahead2(At(0, e))
                phase_b(At(0, e))

            for m, w in enumerate((w_og, w_ig, w_o)):
                sp.dma_start(w_att[:, m, :, :], w).then_inc(w_att_in, 16)
            for e in (NE - 2, NE - 1):
                phase_b(At(0, e))

            def load_v(t):
                sp.dma_start(v_t[:, t.b, :],
                             xn_tiles[bass.ds(t.n(), 1), :, :].rearrange("o p d -> (o p) d")
                             ).then_inc(v_in[t.b], 16)

            def store_res(t):
                sp.wait_ge(c["res_done"], t.n(1))
                for r in range(2):
                    sp.dma_start(out_tiles[bass.ds(t.n(), 1), r, :, :].rearrange("o j d -> (o j) d"),
                                 res[r * SEGQ:(r + 1) * SEGQ, t.b, :]).then_inc(res_out[t.b], 16)

            sp.wait_ge(ye_out[0], 16 * (NE // 2))
            sp.wait_ge(ye_out[1], 16 * (NE // 2))
            load_v(At(0, 0))
            load_v(At(0, 1))
            sp.wait_ge(c["o_ps"], 1)
            sp.wait_ge(c["vT_ps"], 1)
            load_v(At(0, 2))
            with sp.Fori(0, (NT - 4) // 2) as i:
                for off in (1, 2):
                    t = At(i, off)
                    sp.wait_ge(c["o_ps"], t.n(1))
                    load_v(t.plus(2))
                    store_res(t.plus(-1))
            sp.wait_ge(c["o_ps"], NT - 2)
            load_v(At(0, NT - 1))
            for t in (NT - 4, NT - 3, NT - 2, NT - 1):
                store_res(At(0, t))
            for b in range(2):
                sp.wait_ge(res_out[b], 16 * NT)

        @block.gpsimd
        def _(pool):
            nc.gpsimd.iota(slot_row[:, :], [[1, P]], base=0, channel_multiplier=0,
                           allow_small_or_imprecise_dtypes=True).then_inc(s_iota, 1)
            nc.gpsimd.iota(token_row[:, :], [[1, 2], [2, SEGQ]], base=0, channel_multiplier=0,
                           allow_small_or_imprecise_dtypes=True).then_inc(s_iota, 1)
            nc.gpsimd.iota(part_col[:, :], [[1, 1]], base=0, channel_multiplier=1,
                           allow_small_or_imprecise_dtypes=True).then_inc(s_iota, 1)
            nc.gpsimd.iota(head_want[:, :, :], [[0, DC], [1, 2], [2, 2]], base=0, channel_multiplier=0,
                           allow_small_or_imprecise_dtypes=True).then_inc(s_iota, 1)
            nc.gpsimd.iota(token_parts[:, :, 0], [[0, NT]], base=0, channel_multiplier=1,
                           allow_small_or_imprecise_dtypes=True).then_inc(s_iota, 1)
            nc.gpsimd.iota(token_parts[:, :, 1], [[P, NT]], base=0, channel_multiplier=0,
                           allow_small_or_imprecise_dtypes=True).then_inc(s_iota, 1)
            nc.gpsimd.memset(epow[:, :], -0.5).then_inc(s_zero, 1)
            nc.gpsimd.memset(ones_mat[:, :], 1.0).then_inc(s_zero, 1)
            nc.gpsimd.memset(ones_bf[:, :], 1.0).then_inc(s_zero, 1)
            nc.gpsimd.memset(probs[:, :, :], 0.0).then_inc(s_zero, 1)
            nc.gpsimd.memset(msum_bf[:, :], 0.0).then_inc(s_zero, 1)

            def rsqrt(which, ready, added, done, t):
                pool.wait_ge(ready, t.n(1))
                plain()
                nc.gpsimd.tensor_scalar(rstd[:, which, :], mv[:, which, 1:2], EPS, None, ALU.add
                                        ).then_inc(added, 1)
                pool.wait_ge(added, t.n(1))
                nc.gpsimd.tensor_tensor(rstd[:, which, :], rstd[:, which, :], epow[:, :], ALU.pow
                                        ).then_inc(done, 1)

            def plain():
                pool.sem_inc(s_pool_apart, 1)

            pool.wait_ge(s_zero, 5)
            pool.wait_ge(s_c0, 48)

            def norm1(t):
                pool.wait_ge(x_in[t.b], t.dma2())
                if t.past(2):
                    pool.wait_ge(a["x1_done"], t.n(-1))
                nc.gpsimd.tensor_tensor(x_bias[:, t.b, :], xin[:, t.b, :], bias_bc[:, :], ALU.add
                                        ).then_inc(a["xb_done"], 1)
                rsqrt(0, a["stat1"], a["var1"], a["rstd1"], t)

            def norm2(t):
                rsqrt(1, a["stat2"], a["var2"], a["rstd2"], t)

            norm1(At(0, 0))

            def phase_a(t):
                norm1(t.plus(1))
                norm2(t)

            phase_a(At(0, 0))
            with pool.Fori(0, (NT - 2) // 2) as i:
                phase_a(At(i, 1))
                phase_a(At(i, 2))
            norm2(At(0, NT - 1))

            for b in range(2):
                pool.wait_ge(xn_out[b], 16 * (NT // 2))
            pool.wait_ge(a["acc_done"], NT)

            def gather(e, free):
                pool.wait_ge(e_["row_done"], e.n(1))
                if free:
                    pool.wait_ge(e_["xeT_ps"], e.n(-1))
                plain()
                nc.gpsimd.indirect_dma_start(
                    xe[:, e.b, :], None, xn_rows[:, :],
                    bass.IndirectOffsetOnAxis(ap=row_i[:, e.b, :], axis=0)).then_inc(xe_in[e.b], 16)

            gather(At(0, 0), False)
            gather(At(0, 1), False)
            with pool.Fori(0, (NE - 2) // 2) as i:
                gather(At(i, 2), True)
                gather(At(i, 3), True)

            pool.wait_ge(ye_out[0], 16 * (NE // 2))
            pool.wait_ge(ye_out[1], 16 * (NE // 2))

            def gather_rows(t, free):
                for k in range(TOPK):
                    if free:
                        pool.wait_ge(c["gat_used"], (t.n(-1)) * TOPK + (k + 1))
                    plain()
                    nc.gpsimd.indirect_dma_start(
                        gat[:, k, :], None, ye_rows[:, :],
                        bass.IndirectOffsetOnAxis(
                            ap=row_k[:, t.b, k:k + 1], axis=0)
                    ).then_inc(gat_in[k], 16)

            def rsqrt_c(t):
                pool.wait_ge(c["sq_done"], t.n(1))
                if t.past(1):
                    pool.wait_ge(c["og_done"], t.n())
                plain()
                nc.gpsimd.tensor_scalar(orstd, osq, 1.0 / D, EPS, ALU.mult, ALU.add).then_inc(c["ms_done"], 1)
                pool.wait_ge(c["ms_done"], t.n(1))
                nc.gpsimd.tensor_tensor(orstd, orstd, epow[:, :], ALU.pow).then_inc(c["rstd"], 1)

            def copy_rows(t):
                nc.gpsimd.tensor_copy(row_k[:, t.b, :], rows_of[:, bass.ds(t.n(), 1), :]
                                      .rearrange("p o k -> p (o k)")).then_inc(c["row_k"], 1)
                pool.wait_ge(c["row_k"], t.n(1))

            def phase_c(t, free):
                copy_rows(t)
                gather_rows(t, free)
                rsqrt_c(t)

            phase_c(At(0, 0), False)
            phase_c(At(0, 1), True)
            with pool.Fori(0, (NT - 2) // 2) as i:
                phase_c(At(i, 2), True)
                phase_c(At(i, 3), True)

        @block.vector
        def _(dve):
            v = nc.vector
            count = [0]

            def link(ins):
                count[0] += 1
                ins.then_inc(s_const, 1)
                dve.wait_ge(s_const, count[0])

            def plain():
                dve.sem_inc(s_dve_apart, 1)

            class Chain:

                def __init__(self, at, done, k):
                    self.at, self.done, self.k, self.j = at, done, k, 0

                def __call__(self, ins, apart=False):
                    self.j += 1
                    ins.then_inc(self.done, 1)
                    dve.wait_ge(self.done, self.at.n() * self.k + self.j)
                    if apart:
                        plain()

                def end(self):
                    assert self.j == self.k

            v.memset(att, 0.0)
            dve.wait_ge(s_iota, 6)
            v.tensor_scalar(ident[:, :], slot_row[:, :], part_col[:, :], None, ALU.is_equal)
            v.tensor_scalar(ident_bf[:, :], slot_row[:, :], part_col[:, :], None, ALU.is_equal).then_inc(s_set, 1)
            v.tensor_copy(slot_row_bf[:, :], slot_row[:, :])
            link(v.tensor_scalar(tmp_col[:, 0:1], part_col[:, :], float(SEGQ), -float(P - 1), ALU.is_ge, ALU.mult))
            link(v.scalar_tensor_tensor(token_col[:, :], part_col[:, :], 2.0, tmp_col[:, 0:1], ALU.mult, ALU.add))
            v.tensor_scalar(chunk_of[:, 0:1], token_col[:, :], float(SEGQ), None, ALU.is_lt)
            v.tensor_scalar(chunk_of[:, 1:2], token_col[:, :], float(SEGQ), None, ALU.is_ge)
            link(v.tensor_scalar(chunk_col[:, :], token_col[:, :], float(SEGQ), None, ALU.is_ge))
            link(v.tensor_scalar(chunk_row[:, :], token_row[:, :], float(SEGQ), None, ALU.is_ge))
            v.tensor_scalar(before_bf[:, :], token_row[:, :], token_col[:, :], None, ALU.is_gt)
            link(v.tensor_scalar(same_chunk[:, :], chunk_row[:, :], chunk_col[:, :], None, ALU.is_equal))
            link(v.scalar_tensor_tensor(causal[:, :], token_row[:, :], token_col[:, :], same_chunk[:, :],
                                        ALU.is_ge, ALU.mult))
            link(v.scalar_tensor_tensor(tmp_col[:, 1:2], chunk_col[:, :], -float(SEGQ), token_col[:, :],
                                        ALU.mult, ALU.add))
            link(v.tensor_scalar(tmp_col[:, 2:3], tmp_col[:, 1:2], float(SEGQ // 2), None, ALU.is_lt))
            link(v.tensor_scalar(first_half[:, :], same_chunk[:, :], tmp_col[:, 2:3], None, ALU.mult))
            v.tensor_tensor(from_mid[:, :], causal[:, :], first_half[:, :], ALU.subtract)
            v.tensor_tensor(to_last[:, :], same_chunk[:, :], causal[:, :], ALU.subtract)
            link(v.tensor_scalar(tmp_col[:, 0:1], part_col[:, :], 32.0, None, ALU.is_ge))
            link(v.tensor_scalar(tmp_col[:, 1:2], part_col[:, :], 64.0, None, ALU.is_ge))
            link(v.tensor_scalar(tmp_col[:, 2:3], part_col[:, :], 96.0, None, ALU.is_ge))
            link(v.tensor_tensor(tmp_col[:, 3:4], tmp_col[:, 0:1], tmp_col[:, 1:2], ALU.add))
            link(v.tensor_tensor(tmp_col[:, 0:1], tmp_col[:, 3:4], tmp_col[:, 2:3], ALU.add))
            v.tensor_scalar(head_rows[:, :, :], head_want[:, :, :], tmp_col[:, 0:1], None, ALU.is_equal)

            def norm1(t):
                ln = Chain(t, a["ln_steps"], 5)
                dve.wait_ge(x_in[t.b], t.dma2())
                ln(v.bn_stats(stats[:, 0, :], xin[:, t.b, :]), apart=True)
                v.bn_aggr(mv[:, 0, :], stats[:, 0, :]).then_inc(a["stat1"], 1)
                dve.wait_ge(a["rstd1"], t.n(1))
                if t.past(2):
                    dve.wait_ge(a["att_ps"], t.n(-1))
                v.tensor_scalar(xn[:, t.b, :], xin[:, t.b, :], mv[:, 0, 0:1], rstd[:, 0, :],
                                ALU.subtract, ALU.mult).then_inc(a["xn_done"], 1)
                dve.wait_ge(a["xn_done"], t.n(1))
                ln(v.tensor_reduce(xmax[:, :], xn[:, t.b, :], AX.X, ALU.max, apply_absolute_value=True))
                ln(v.tensor_scalar(xscale[:, t.b, :], xmax[:, :], 1.0 / QMAX, 1e-12, ALU.mult, ALU.max))
                ln(v.reciprocal(xinv[:, :], xscale[:, t.b, :]))
                ln(v.tensor_scalar(xq_f, xn[:, t.b, :], xinv[:, :], MAGIC, ALU.mult, ALU.add))
                if t.past(1):
                    dve.wait_ge(a["xqT_ps"], t.n())
                v.tensor_scalar(xq[:, :], xq_f, MAGIC, None, ALU.subtract).then_inc(a["xq_done"], 1)
                ln.end()

            def spread_heads(t):
                dve.wait_ge(a["xnT_sb"], t.n(1))
                if t.past(1):
                    dve.wait_ge(a["s_ps"], t.n())
                src = xnT.rearrange("p c (r o j) -> p (c r) o j", r=2, o=1)
                v.tensor_tensor(xn_heads, src.to_broadcast([P, 2 * DC, 2, SEGQ]),
                                head_rows[:, :, :].unsqueeze(3).to_broadcast([P, 2 * DC, 2, SEGQ]), ALU.mult
                                ).then_inc(a["xnh_done"], 1)

            def router_max(t):
                dve.wait_ge(a["lg_sb"], t.n(1))
                if t.past(1):
                    dve.wait_ge(a["gexp_done"], t.n())
                v.tensor_reduce(gmax[:, :], glog[:, :], AX.X, ALU.max, negate=True
                                ).then_inc(a["gmax_done"], 1)

            def scores(t):
                dve.wait_ge(a["s_ps"], t.n(1))
                s = bank[2][:, :].rearrange("p (h j) -> p h j", h=HP)
                v.tensor_reduce(smax[:, :], s, AX.X, ALU.max).then_inc(a["smax_done"], 1)
                dve.wait_ge(a["smax_done"], t.n(1))
                if t.past(1):
                    dve.wait_ge(a["exp_done"], t.n())
                v.tensor_tensor(dist, s, smax[:, :].unsqueeze(2).to_broadcast([P, HP, SEGQ]), ALU.subtract
                                ).then_inc(a["dist_done"], 1)

            def gate_half(t, half):
                dve.wait_ge(a["silA" if half == 0 else "silB"], t.n(1))
                dve.wait_ge(a["wb_ps" if half == 0 else "wd_ps"], t.n(1))
                part = hs[:, half * SQ:(half + 1) * SQ]
                v.tensor_tensor(part, part, bank[7][:, 0:SQ], ALU.mult
                                ).then_inc(a["hA_done" if half == 0 else "hB_done"], 1)

            def top_experts(t):
                rt = Chain(t, a["rt_steps"], 6)
                dve.wait_ge(a["gexp_done"], t.n(1))
                rt(v.reciprocal(ginv[:, :], gsum[:, :]))
                rt(v.tensor_scalar(score[:, :], gexp[:, :], ginv[:, :], None, ALU.mult), apart=True)
                rt(v.max(top_v[:, :], score[:, :]), apart=True)
                rt(v.max_index(top_i[:, :], top_v[:, :], score[:, :]))
                rt(v.tensor_copy(top_f[:, :], top_i[:, :]))
                rt(v.tensor_tensor(chosen[:, :, :], slot_row[:, 0:NE].unsqueeze(1).to_broadcast([P, TOPK, NE]),
                                   top_f[:, 0:TOPK].unsqueeze(2).to_broadcast([P, TOPK, NE]), ALU.is_equal))
                if t.past(1):
                    dve.wait_ge(a["pos_ps"], t.n())
                with nc.allow_low_precision(reason="zeros and ones"):
                    v.tensor_reduce(mask_bf[:, :], chosen[:, :, :].rearrange("p k e -> p e k"), AX.X, ALU.add
                                    ).then_inc(a["mask_done"], 1)
                rt.end()

            def slots(t):
                sl = Chain(t, a["slot_steps"], 8)
                dve.wait_ge(a["pos_ps"], t.n(1))
                dve.wait_ge(a["mask_done"], t.n(1))
                pos = bank[1][:, 384:384 + NE]
                sl(v.tensor_tensor(msum_bf[:, :], msum_bf[:, :], mask_bf[:, :], ALU.add))
                sl(v.scalar_tensor_tensor(posm_f[:, :], pos, 1.0, mask_bf[:, :], ALU.add, ALU.mult))
                sl(v.tensor_scalar(posm[:, :, bass.ds(t.n(), 1)].rearrange("p e o -> p (e o)"), posm_f[:, :],
                                   -1.0, None, ALU.add))
                sl(v.tensor_tensor(chosen_pos[:, :, :], chosen[:, :, :],
                                   pos.unsqueeze(1).to_broadcast([P, TOPK, NE]), ALU.mult))
                sl(v.tensor_reduce(pos_k[:, :], chosen_pos[:, :, :], AX.X, ALU.add))
                v.tensor_scalar(keep[:, :], pos_k[:, :], float(CAP), None, ALU.is_lt)
                sl(v.tensor_scalar(pos_c[:, :], pos_k[:, :], float(CAP - 1), None, ALU.min))
                sl(v.tensor_tensor(gates[:, bass.ds(t.n(), 1), :].rearrange("p o k -> p (o k)"),
                                   top_v[:, 0:TOPK], keep[:, :], ALU.mult))
                sl(v.scalar_tensor_tensor(rows_of[:, bass.ds(t.n(), 1), :].rearrange("p o k -> p (o k)"),
                                          top_f[:, 0:TOPK], float(CAP), pos_c[:, :], ALU.mult, ALU.add))
                sl.end()

            def sums(t):
                dve.wait_ge(a["exp_done"], t.n(1))
                v.tensor_reduce(esum[:, :], probs[:, :, :], AX.X, ALU.add).then_inc(a["esum_done"], 1)
                dve.wait_ge(a["esum_done"], t.n(1))
                v.reciprocal(einv[:, :], esum[:, :])

            def residual(t):
                su = Chain(t, a["sum_steps"], 5)
                dve.wait_ge(a["f_ps"], t.n(1))
                su(v.scalar_tensor_tensor(y, bank[3][:, :], xscale[:, t.b, :], wscale_bc[:, :], ALU.mult, ALU.mult))
                dve.wait_ge(a["xb_done"], t.n(1))
                su(v.tensor_tensor(y, y, x_bias[:, t.b, :], ALU.add))
                dve.wait_ge(a["att_ps"], t.n(1))
                o = bank[2][:, :].rearrange("p (h r d) -> p h r d", h=HP, r=2)
                su(v.tensor_tensor(att[0:SEGQ, :, 0, :], o[0:SEGQ, :, 0, :],
                                   einv[0:SEGQ, :].unsqueeze(2).to_broadcast([SEGQ, HP, HD]), ALU.mult))
                su(v.tensor_tensor(att[SEGQ:P, :, 1, :], o[SEGQ:P, :, 1, :],
                                   einv[SEGQ:P, :].unsqueeze(2).to_broadcast([SEGQ, HP, HD]), ALU.mult))
                v.tensor_tensor(x1[:, t.b, :], y, att.rearrange("p h r d -> p (h r d)"), ALU.add
                                ).then_inc(a["x1_done"], 1)
                dve.wait_ge(a["x1_done"], t.n(1))
                su(v.bn_stats(stats[:, 1, :], x1[:, t.b, :]), apart=True)
                v.bn_aggr(mv[:, 1, :], stats[:, 1, :]).then_inc(a["stat2"], 1)
                dve.wait_ge(a["rstd2"], t.n(1))
                if t.past(2):
                    dve.wait_ge(xn_out[t.b], t.dma(1))
                    dve.wait_ge(a["xn2T_ps"], t.n(-1))
                v.tensor_scalar(xn2[:, t.b, :], x1[:, t.b, :], mv[:, 1, 0:1], rstd[:, 1, :],
                                ALU.subtract, ALU.mult).then_inc(a["xn2_done"], 1)
                su.end()

            def keep_sum(t):
                dve.wait_ge(a["z_ps"], t.n(1))
                v.tensor_tensor(acc[:, bass.ds(t.n(), 1), :].rearrange("p o d -> p (o d)"),
                                x1[:, t.b, :], bank[6][:, :], ALU.add).then_inc(a["acc_done"], 1)

            norm1(At(0, 0))

            dve.wait_ge(s_wn, 16)
            link(v.tensor_reduce(wcols[:, 0, :], wn, AX.X, ALU.max, apply_absolute_value=True))
            link(v.tensor_scalar(wcols[:, 0, :], wcols[:, 0, :], 1e-8, None, ALU.max))
            link(v.tensor_scalar(wcols[:, 1, :], wcols[:, 0, :], 1.0 / QMAX, None, ALU.mult))
            link(v.reciprocal(wcols[:, 2, :], wcols[:, 1, :]))
            for k in range(DC):
                link(v.tensor_scalar(wn[:, k, :], wn[:, k, :], wcols[:, 2, k:k + 1], MAGIC, ALU.mult, ALU.add))
                v.tensor_scalar(wq[:, k, :], wn[:, k, :], MAGIC, None, ALU.subtract).then_inc(s_wq, 1)
                v.tensor_scalar(wdiag[:, k, :], ident[:, :], wcols[:, 1, k:k + 1], None, ALU.mult).then_inc(s_wq, 1)

            def phase_a(at):
                if at.cur:
                    spread_heads(at.cur)
                if at.prev:
                    router_max(at.prev)
                if at.cur:
                    scores(at.cur)
                if at.prev:
                    gate_half(at.prev, 0)
                    top_experts(at.prev)
                if at.next:
                    norm1(at.next)
                if at.cur:
                    sums(at.cur)
                if at.prev:
                    gate_half(at.prev, 1)
                    slots(at.prev)
                if at.cur:
                    residual(at.cur)
                if at.prev:
                    keep_sum(at.prev)

            dve.wait_ge(s_wsb, 1)
            dve.wait_ge(s_zero, 5)
            turns(dve, NT, phase_a, 1)

            def one_hot(e):
                if e.past(1):
                    dve.wait_ge(e_["slot_ps"], e.n())
                v.tensor_tensor(hot[:, :, :], slot_row_bf[:, :].unsqueeze(1).to_broadcast([P, NT, CAP]),
                                posm[:, bass.ds(e.n(), 1), :].rearrange("p o t -> p (o t)").unsqueeze(2)
                                .to_broadcast([P, NT, CAP]), ALU.is_equal).then_inc(e_["hot_done"], 1)

            def slot_rows(e):
                dve.wait_ge(e_["slot_ps"], e.n(1))
                if e.past(2):
                    dve.wait_ge(xe_in[e.b], e.dma(1))
                with nc.allow_low_precision(reason="whole numbers below 2**24"):
                    v.tensor_reduce(row_i[:, e.b, :], bank[5][:, 0:2], AX.X, ALU.add).then_inc(e_["row_done"], 1)

            def gate_expert(e):
                dve.wait_ge(e_["sil_done"], e.n(1))
                dve.wait_ge(e_["h3_ps"], e.n(1))
                if e.past(2):
                    dve.wait_ge(e_["hT_ps"], e.n(-1))
                v.tensor_tensor(he[:, e.b, :], hsil, bank[1][:, 0:IE], ALU.mult).then_inc(e_["h_done"], 1)

            for k in range(2):
                one_hot(At(0, k))
                slot_rows(At(0, k))

            def phase_b(at):
                if at.after:
                    one_hot(at.after)
                if at.cur:
                    gate_expert(at.cur)
                if at.after:
                    slot_rows(at.after)

            turns(dve, NE, phase_b, 3)

            dve.wait_ge(e_["y_sb"], NE)
            v.memset(state[0:DK, 0, :], 0.0)

            def lg(t, part):
                return qk_logits[:, bass.ds(t.n(), 1), part * DK:(part + 1) * DK].rearrange("p o k -> p (o k)")

            def q_max(t):
                if t.past(1):
                    dve.wait_ge(c["eq_done"], t.n())
                v.tensor_scalar(klog, lg(t, 1), -88.0, None, ALU.max)
                v.tensor_reduce(qmaxn, lg(t, 0), AX.X, ALU.max, negate=True).then_inc(c["qmax"], 1)

            def q_and_k(t):
                st = Chain(t, c["qk_steps"], 3)
                dve.wait_ge(c["eq_done"], t.n(1))
                st(v.reciprocal(qinv, qsum))
                st(v.tensor_scalar(qk[:, 0, :], softq, qinv, None, ALU.mult))
                dve.wait_ge(c["kexp_done"], t.n(1))
                st(v.tensor_scalar(kexp, kexp, 1.0, None, ALU.add))
                st.end()
                v.reciprocal(qk[:, 1, :], kexp).then_inc(c["qk_done"], 1)

            def decayed(t):
                dve.wait_ge(c["ex_done"], t.n(1))
                dve.wait_ge(c["exm_done"], t.n(1))
                dve.wait_ge(c["qk_done"], t.n(1))
                if t.past(1):
                    dve.wait_ge(c["gT_ps"], t.n())
                    dve.wait_ge(c["ds_ps"], t.n())
                v.tensor_tensor(q_mid, qk[:, 0, :], ex[:, 0, :], ALU.mult)
                v.tensor_tensor(k_mid, qk[:, 1, :], exm, ALU.mult)
                v.tensor_copy(decay, ex[:, 3:4, :].to_broadcast([P, 2, DK]))
                v.tensor_tensor(qk_e, qk, ex[:, 1:3, :], ALU.mult).then_inc(c["qk_e"], 1)
                dve.wait_ge(c["qk_e"], t.n(1))
                v.tensor_tensor(qk_c, qk_e.unsqueeze(2).to_broadcast([P, 2, 2, DK]),
                                chunk_of[:, :].unsqueeze(1).unsqueeze(3).to_broadcast([P, 2, 2, DK]), ALU.mult
                                ).then_inc(c["nat_done"], 1)

            def mask_att(t):
                dve.wait_ge(c["at_ps"], t.n(1))
                if t.past(1):
                    dve.wait_ge(c["o_ps"], t.n())
                v.tensor_tensor(attT, bank[0][:, 0:P], causal[:, :], ALU.mult).then_inc(c["at_sb"], 1)

            def state_mid(t):
                dve.wait_ge(c["ds_ps"], t.n(1))
                dve.wait_ge(c["gT_sb"], t.n(1))
                if t.past(1):
                    dve.wait_ge(c["s_next"], t.n())
                v.scalar_tensor_tensor(state[DK:2 * DK, t.b, :], state[0:DK, t.b, :], att_l[0:DK, 3, 0:1],
                                       bank[1][0:DK, :], ALU.mult, ALU.add).then_inc(c["s_mid"], 1)

            def state_next(t):
                dve.wait_ge(c["s_mid"], t.n(1))
                v.scalar_tensor_tensor(state[0:DK, 1 - t.b, :], state[DK:2 * DK, t.b, :],
                                       att_l[DK:2 * DK, 3, DK:DK + 1], bank[1][DK:2 * DK, :],
                                       ALU.mult, ALU.add).then_inc(c["s_next"], 1)

            def o_out(t):
                dve.wait_ge(c["o_ps"], t.n(1))
                if t.past(1):
                    dve.wait_ge(c["oT_ps"], t.n())
                    dve.wait_ge(c["sq_done"], t.n())
                v.tensor_copy(o_sb, bank[2][:, :]).then_inc(c["o_sb"], 1)

            def gated(t):
                dve.wait_ge(c["rstd"], t.n(1))
                dve.wait_ge(c["sil_done"], t.n(1))
                if t.past(1):
                    dve.wait_ge(c["ogT_ps"], t.n())
                v.scalar_tensor_tensor(og, o_sb, orstd, sil, ALU.mult, ALU.mult).then_inc(c["og_done"], 1)

            def gatedT(t):
                dve.wait_ge(c["ogT_ps"], t.n(1))
                if t.past(1):
                    dve.wait_ge(c["out_ps"], t.n())
                v.tensor_tensor(ogT, split4(bank[3]), gnorm[:, :].unsqueeze(2).to_broadcast([P, DC, P]), ALU.mult
                                ).then_inc(c["ogT_sb"], 1)

            def add_experts(t):
                for k in range(TOPK):
                    before = (acc[:, bass.ds(t.n(), 1), :].rearrange("p o d -> p (o d)") if k == 0
                              else racc[:, t.b, :])
                    dve.wait_ge(gat_in[k], t.i * 32 + 16 * (t.off + 1))
                    if k:
                        dve.wait_ge(c["gat_used"], t.n() * TOPK + k)
                    v.scalar_tensor_tensor(racc[:, t.b, :], gat[:, k, :],
                                           gates[:, bass.ds(t.n(), 1), k:k + 1].rearrange("p o k -> p (o k)"),
                                           before, ALU.mult, ALU.add).then_inc(c["gat_used"], 1)

            def result(t):
                dve.wait_ge(c["out_ps"], t.n(1))
                dve.wait_ge(c["gat_used"], t.n(1) * TOPK)
                if t.past(2):
                    dve.wait_ge(res_out[t.b], t.i * 32 + 32 * (t.off // 2))
                v.tensor_tensor(res[:, t.b, :], racc[:, t.b, :], bank[7][:, :], ALU.add).then_inc(c["res_done"], 1)

            q_max(At(0, 0))
            q_and_k(At(0, 0))
            decayed(At(0, 0))

            def phase_c(at):
                if at.cur:
                    mask_att(at.cur)
                if at.next:
                    q_max(at.next)
                if at.cur:
                    state_mid(at.cur)
                if at.next:
                    q_and_k(at.next)
                if at.cur:
                    state_next(at.cur)
                if at.prev:
                    gatedT(at.prev)
                if at.next:
                    decayed(at.next)
                if at.cur:
                    o_out(at.cur)
                if at.prev:
                    result(at.prev)
                if at.cur:
                    add_experts(at.cur)
                    gated(at.cur)

            turns(dve, NT, phase_c, 1)

        @block.scalar
        def _(act):
            s = nc.scalar

            def copy(out, in_):
                return s.activation(out, in_, ACT.Copy)

            for m in range(DC):
                act.wait_ge(s_wqT, m + 1)
                last = copy(wqT[:, m, :], bank[m][:, 0:256].bitcast(bf16))
            last.then_inc(s_wqe, 1)
            act.wait_ge(s_wqT, DC + 1)
            copy(wscale_bc[:, :], bank[4][:, :]).then_inc(s_wsb, 1)

            def xn2T_out(t):
                act.wait_ge(a["xn2T_ps"], t.n(1))
                if t.past(1):
                    act.wait_ge(a["wd_ps"], t.n())
                copy(xn2T, split4(bank[0])).then_inc(a["xn2T_sb"], 1)

            def xT_out(t):
                act.wait_ge(a["xqT_ps"], t.n(1))
                if t.past(1):
                    act.wait_ge(a["f_ps"], t.n())
                copy(xqT[:, :, :], bank[1][:, 0:256].bitcast(bf16).rearrange("p (c k) -> p c k", c=DC)
                     ).then_inc(a["xqT_sb"], 1)
                act.wait_ge(a["xnT_ps"], t.n(1))
                if t.past(1):
                    act.wait_ge(a["s_ps"], t.n())
                copy(xnT, split4(bank[0])).then_inc(a["xnT_sb"], 1)

            def router_exp(t):
                act.wait_ge(a["lg_ps"], t.n(1))
                if t.past(1):
                    act.wait_ge(a["gmax_done"], t.n())
                copy(qk_logits[:, bass.ds(t.n(), 1), :].rearrange("p o k -> p (o k)"),
                     bank[1][:, 256 + NE:256 + NE + 2 * DK])
                copy(glog[:, :], bank[1][:, 256:256 + NE]).then_inc(a["lg_sb"], 1)
                act.wait_ge(a["gmax_done"], t.n(1))
                if t.past(1):
                    act.wait_ge(a["mask_done"], t.n())
                s.activation(gexp[:, :], glog[:, :], ACT.Exp, bias=gmax[:, :], accum_out=gsum[:, :]
                             ).then_inc(a["gexp_done"], 1)

            def att_exp(t):
                act.wait_ge(a["dist_done"], t.n(1))
                if t.past(1):
                    act.wait_ge(a["eT_ps1"], t.n())
                    act.wait_ge(a["esum_done"], t.n())
                s.activation(probs[0:SEGQ, :, 0:SEGQ], dist[0:SEGQ, :, :], ACT.Exp, scale=ATT_SCALE)
                s.activation(probs[SEGQ:P, :, SEGQ:P], dist[SEGQ:P, :, :], ACT.Exp, scale=ATT_SCALE
                             ).then_inc(a["exp_done"], 1)

            def silu_half(t, half):
                act.wait_ge(a["wa_ps" if half == 0 else "wc_ps"], t.n(1))
                if half == 0 and t.past(1):
                    act.wait_ge(a["hT_ps"], t.n())
                s.activation(hs[:, half * SQ:(half + 1) * SQ], bank[6][:, 0:SQ], ACT.Silu
                             ).then_inc(a["silA" if half == 0 else "silB"], 1)

            def eT_out(t):
                if t.past(1):
                    act.wait_ge(a["att_ps"], t.n())
                act.wait_ge(a["eT_ps0"], t.n(1))
                copy(eT[:, 0:4, :], split4(bank[4]))
                act.wait_ge(a["eT_ps1"], t.n(1))
                copy(eT[:, 4:8, :], split4(bank[5])).then_inc(a["eT_sb"], 1)

            def hsT_out(t):
                act.wait_ge(a["hT_ps"], t.n(1))
                if t.past(1):
                    act.wait_ge(a["z_ps"], t.n())
                copy(hsT[:, 0:4, :], split4(bank[4]))
                copy(hsT[:, 4, :], bank[5][:, 0:P])
                copy(hsT[0:SR, 5, :], bank[5][0:SR, P:2 * P]).then_inc(a["hT_sb"], 1)

            def phase_a(at):
                if at.prev:
                    xn2T_out(at.prev)
                if at.cur:
                    xT_out(at.cur)
                if at.prev:
                    router_exp(at.prev)
                if at.cur:
                    att_exp(at.cur)
                if at.prev:
                    silu_half(at.prev, 0)
                    silu_half(at.prev, 1)
                if at.cur:
                    eT_out(at.cur)
                if at.prev:
                    hsT_out(at.prev)

            act.wait_ge(s_zero, 5)
            turns(act, NT, phase_a, 1)

            act.wait_ge(a["acc_done"], NT)

            def silu_expert(e):
                act.wait_ge(e_["h1_ps"], e.n(1))
                if e.past(1):
                    act.wait_ge(e_["h_done"], e.n())
                s.activation(hsil, bank[0][:, 0:IE], ACT.Silu).then_inc(e_["sil_done"], 1)

            def heT_out(e):
                act.wait_ge(e_["hT_ps"], e.n(1))
                if e.past(1):
                    act.wait_ge(e_["y_ps"], e.n())
                copy(heT[:, 0:2, :], bank[3][:, 0:2 * P].rearrange("p (c k) -> p c k", c=2))
                copy(heT[0:IB, 2, :], bank[3][0:IB, 2 * P:3 * P]).then_inc(e_["hT_sb"], 1)

            def xeT_out(e):
                act.wait_ge(e_["xeT_ps"], e.n(1))
                if e.past(2):
                    act.wait_ge(e_["h3_ps"], e.n(-1))
                copy(xeT[:, e.b, :, :], split4(bank[2])).then_inc(e_["xeT_sb"], 1)

            def ye_sb(e):
                act.wait_ge(e_["y_ps"], e.n(1))
                if e.past(2):
                    act.wait_ge(ye_out[e.b], e.dma(1))
                copy(ye[:, e.b, :], bank[4][:, :]).then_inc(e_["y_sb"], 1)

            xeT_out(At(0, 0))

            def phase_b(at):
                if at.cur:
                    silu_expert(at.cur)
                if at.prev:
                    heT_out(at.prev)
                if at.next:
                    xeT_out(at.next)
                if at.prev:
                    ye_sb(at.prev)

            turns(act, NE, phase_b, 3)

            act.wait_ge(ye_out[0], 16 * (NE // 2))
            act.wait_ge(ye_out[1], 16 * (NE // 2))

            def lg(t, part):
                return qk_logits[:, bass.ds(t.n(), 1), part * DK:(part + 1) * DK].rearrange("p o k -> p (o k)")

            def exps(t):
                if t.past(1):
                    act.wait_ge(c["qk_done"], t.n())
                act.wait_ge(c["qmax"], t.n(1))
                s.activation(kexp, klog, ACT.Exp, scale=-1.0).then_inc(c["kexp_done"], 1)
                s.activation(softq, lg(t, 0), ACT.Exp, bias=qmaxn, accum_out=qsum).then_inc(c["eq_done"], 1)

            def log_gate(t):
                act.wait_ge(c["qk_done"], t.n(1))
                s.activation(kgate, qk[:, 1, :], ACT.Exp).then_inc(c["kgate_done"], 1)
                act.wait_ge(c["kgate_done"], t.n(1))
                if t.past(1):
                    act.wait_ge(c["cum_ps"], t.n())
                s.activation(gfn, kgate, ACT.Ln, bias=1.0).then_inc(c["gf_done"], 1)

            def decays(t):
                act.wait_ge(c["cum_ps"], t.n(1))
                if t.past(1):
                    act.wait_ge(c["nat_done"], t.n())
                cum = bank[5][:, 0:P].rearrange("p (m k) -> p m k", m=4)
                s.activation(ex, cum, ACT.Exp, scale=-1.0).then_inc(c["ex_done"], 1)
                s.activation(exm, cum[:, 0, :], ACT.Exp).then_inc(c["exm_done"], 1)

            def square(t):
                act.wait_ge(c["o_sb"], t.n(1))
                if t.past(1):
                    act.wait_ge(c["og_done"], t.n())
                s.activation(sil, o_sb, ACT.Square, accum_out=osq).then_inc(c["sq_done"], 1)

            def oT_out(t):
                act.wait_ge(c["oT_ps"], t.n(1))
                if t.past(1):
                    act.wait_ge(c["go_ps"], t.n())
                copy(oT, split4(bank[3])).then_inc(c["oT_sb"], 1)

            def gT_out(t):
                act.wait_ge(c["gT_ps"], t.n(1))
                if t.past(1):
                    act.wait_ge(c["o_ps"], t.n())
                    act.wait_ge(c["s_next"], t.n())
                copy(att_l[0:DK, 0:2, :], split4(bank[6])[0:DK, 0:2, :])
                copy(att_l[0:2 * DK, 2:4, :], split4(bank[6])[0:2 * DK, 2:4, :]).then_inc(c["gT_sb"], 1)

            def silu_gate(t):
                act.wait_ge(c["go_ps"], t.n(1))
                act.wait_ge(c["sq_done"], t.n(1))
                s.activation(sil, bank[4][:, :], ACT.Silu).then_inc(c["sil_done"], 1)

            def vT_out(t):
                act.wait_ge(c["vT_ps"], t.n(1))
                if t.past(1):
                    act.wait_ge(c["wig_ps"], t.n())
                copy(vT, split4(bank[5])).then_inc(c["vT_sb"], 1)

            exps(At(0, 0))
            log_gate(At(0, 0))
            decays(At(0, 0))
            gT_out(At(0, 0))
            vT_out(At(0, 0))

            def phase_c(at):
                if at.next:
                    exps(at.next)
                    log_gate(at.next)
                    decays(at.next)
                if at.cur:
                    square(at.cur)
                    oT_out(at.cur)
                if at.next:
                    gT_out(at.next)
                if at.cur:
                    silu_gate(at.cur)
                if at.next:
                    vT_out(at.next)

            turns(act, NT, phase_c, 1)

        @block.tensor
        def _(pe):
            te = nc.tensor

            def chunks(out, lhsT, rhs, n, first=True, last=True):
                for k in range(n):
                    ins = te.matmul(out, lhsT(k), rhs(k), start=first and k == 0, stop=last and k == n - 1)
                return ins

            def transposes(b, src, n=DC):
                for k in range(n):
                    ins = te.transpose(bank[b][:, k * P:(k + 1) * P], src[:, k * P:(k + 1) * P], ident[:, :])
                return ins

            pe.wait_ge(s_set, 1)
            pe.wait_ge(s_zero, 5)
            pe.wait_ge(s_wq, 2 * DC)
            for m in range(DC):
                o = bank[m][:, 0:256].bitcast(bf16)
                for k in range(DC):
                    ins = te.transpose(o[:, k * P:(k + 1) * P], wq[:, k, m * P:(m + 1) * P], ident_bf[:, :])
                ins.then_inc(s_wqT, 1)
            te.matmul(bank[4][:, :], ones_mat[:, :], wdiag.rearrange("p c k -> p (c k)"), start=True, stop=True
                      ).then_inc(s_wqT, 1)
            pe.wait_ge(s_wqe, 1)
            pe.wait_ge(s_wsb, 1)
            pe.wait_ge(s_c0, 48)
            pe.wait_ge(s_const, 1)

            xqT_ps = bank[1][:, 0:256].bitcast(bf16)
            lg_ps = bank[1][:, 256:256 + P]
            pos_ps = bank[1][:, 384:384 + NE]

            def xn2_T(t):
                pe.wait_ge(a["xn2_done"], t.n(1))
                pe.wait_ge(a["xnT_sb"], t.n(1))
                transposes(0, xn2[:, t.b, :]).then_inc(a["xn2T_ps"], 1)

            def x_T(t):
                pe.wait_ge(a["xq_done"], t.n(1))
                if t.past(2):
                    pe.wait_ge(a["slot_steps"], t.n(-1) * 8)
                elif t.past(1):
                    pe.wait_ge(a["xqT_sb"], 1)
                for k in range(DC):
                    ins = te.transpose(xqT_ps[:, k * P:(k + 1) * P], xq[:, k * P:(k + 1) * P], ident_bf[:, :])
                ins.then_inc(a["xqT_ps"], 1)
                pe.wait_ge(a["xn_done"], t.n(1))
                if t.past(1):
                    pe.wait_ge(a["xn2T_sb"], t.n())
                transposes(0, xn[:, t.b, :]).then_inc(a["xnT_ps"], 1)

            def logits(t, with_cur):
                pe.wait_ge(a["xn2T_sb"], t.n(1))
                pe.wait_ge(a["xqT_sb"], t.n(2) if with_cur else t.n(1))
                if t.past(1):
                    pe.wait_ge(a["slot_steps"], t.n() * 8)
                chunks(lg_ps, lambda k: xn2T[:, k, :], lambda k: wrqk[:, k, :], DC).then_inc(a["lg_ps"], 1)

            def shared(t, b, part, done):
                chunks(bank[b][:, 0:SQ], lambda k: xn2T[:, k, :],
                       lambda k: wsh13[:, k, part * SQ:(part + 1) * SQ], DC).then_inc(a[done], 1)

            def att_scores(t):
                pe.wait_ge(a["xnT_sb"], t.n(1))
                pe.wait_ge(a["xnh_done"], t.n(1))
                if t.past(1):
                    pe.wait_ge(a["x1_done"], t.n())
                for k in range(DC):
                    for r in range(2):
                        ins = te.matmul(bank[2][r * SEGQ:(r + 1) * SEGQ, k * P:(k + 1) * P],
                                        xnT[:, k, r * SEGQ:(r + 1) * SEGQ],
                                        xn_heads[:, 2 * k + r, :, :].rearrange("p h j -> p (h j)"),
                                        start=True, stop=True)
                ins.then_inc(a["s_ps"], 1)

            def quantised(t):
                pe.wait_ge(a["xqT_sb"], t.n(1))
                if t.past(1):
                    pe.wait_ge(a["x1_done"], t.n())
                chunks(bank[3][:, :], lambda k: xqT[:, k, :], lambda k: wqT[:, k, :], DC).then_inc(a["f_ps"], 1)

            def positions(t):
                pe.wait_ge(a["mask_done"], t.n(1))
                pe.wait_ge(a["lg_sb"], t.n(1))
                if t.past(1):
                    pe.wait_ge(a["slot_steps"], t.n() * 8)
                te.matmul(pos_ps, before_bf[:, :], mask_bf[:, :], start=True, stop=False)
                te.matmul(pos_ps, ones_bf[:, :], msum_bf[:, :], start=False, stop=True).then_inc(a["pos_ps"], 1)

            def probs_T(t):
                pe.wait_ge(a["exp_done"], t.n(1))
                if t.past(2):
                    pe.wait_ge(a["hT_sb"], t.n(-1))
                for half in range(2):
                    for k in range(4):
                        ins = te.transpose(bank[4 + half][:, k * P:(k + 1) * P], probs[:, 4 * half + k, :],
                                           ident[:, :])
                    ins.then_inc(a[f"eT_ps{half}"], 1)

            def attention(t):
                pe.wait_ge(a["eT_sb"], t.n(1))
                pe.wait_ge(a["dist_done"], t.n(1))
                for k in range(HP):
                    ins = te.matmul(bank[2][:, k * 2 * HD:(k + 1) * 2 * HD], eT[:, k, :],
                                    xn[:, t.b, k * 2 * HD:(k + 1) * 2 * HD], start=True, stop=True)
                ins.then_inc(a["att_ps"], 1)

            def h_T(t, with_cur):
                pe.wait_ge(a["hB_done"], t.n(1))
                pe.wait_ge(a["hA_done"], t.n(1))
                pe.wait_ge(a["eT_sb"], t.n(2) if with_cur else t.n(1))
                for k in range(SC):
                    w = P if k < SC - 1 else SR
                    ins = te.transpose(bank[4 + k // 4][0:w, (k % 4) * P:(k % 4 + 1) * P],
                                       hs[:, k * P:k * P + w], ident[:, :])
                ins.then_inc(a["hT_ps"], 1)

            def shared_out(t):
                pe.wait_ge(a["hT_sb"], t.n(1))
                pe.wait_ge(a["silB"], t.n(1))
                for k in range(SC):
                    w = P if k < SC - 1 else SR
                    ins = te.matmul(bank[6][:, :], hsT[0:w, k, :], wsh2[0:w, k, :], start=k == 0, stop=k == SC - 1)
                ins.then_inc(a["z_ps"], 1)

            def phase_a(at):
                t, p = at.cur, at.prev
                if p:
                    xn2_T(p)
                if t:
                    x_T(t)
                if p:
                    if p.past(1):
                        pe.wait_ge(a["acc_done"], p.n())
                    pe.wait_ge(s_wsh, 48)
                    pe.wait_ge(a["xn2T_sb"], p.n(1))
                    shared(p, 6, 0, "wa_ps")
                    logits(p, t is not None)
                if t:
                    att_scores(t)
                if p:
                    if p.past(1):
                        pe.wait_ge(a["hB_done"], p.n())
                    shared(p, 7, 2, "wb_ps")
                    pe.wait_ge(a["silA"], p.n(1))
                    shared(p, 6, 1, "wc_ps")
                if t:
                    quantised(t)
                if p:
                    positions(p)
                    pe.wait_ge(a["hA_done"], p.n(1))
                    shared(p, 7, 3, "wd_ps")
                if t:
                    probs_T(t)
                    attention(t)
                if p:
                    h_T(p, t is not None)
                    shared_out(p)

            turns(pe, NT, phase_a, 1)

            pe.wait_ge(a["acc_done"], NT)
            pe.wait_ge(a["slot_steps"], 8 * NT)

            def slot_table(e):
                pe.wait_ge(e_["hot_done"], e.n(1))
                if e.past(1):
                    pe.wait_ge(e_["row_done"], e.n())
                chunks(bank[5][:, 0:2], lambda k: hot[:, k, :], lambda k: token_parts[:, k, :], NT
                       ).then_inc(e_["slot_ps"], 1)

            def xe_T(e):
                pe.wait_ge(xe_in[e.b], e.dma())
                if e.past(1):
                    pe.wait_ge(e_["xeT_sb"], e.n())
                transposes(2, xe[:, e.b, :]).then_inc(e_["xeT_ps"], 1)

            def first(e):
                pe.wait_ge(e_["xeT_sb"], e.n(1))
                pe.wait_ge(w13_in[e.b], e.dma())
                if e.past(1):
                    pe.wait_ge(e_["sil_done"], e.n())
                chunks(bank[0][:, 0:IE], lambda k: xeT[:, e.b, k, :], lambda k: w13_sb[:, e.b, k, 0:IE], DC
                       ).then_inc(e_["h1_ps"], 1)
                if e.past(1):
                    pe.wait_ge(e_["h_done"], e.n())
                chunks(bank[1][:, 0:IE], lambda k: xeT[:, e.b, k, :], lambda k: w13_sb[:, e.b, k, IE:I2], DC
                       ).then_inc(e_["h3_ps"], 1)

            def he_T(e):
                pe.wait_ge(e_["h_done"], e.n(1))
                if e.past(1):
                    pe.wait_ge(e_["hT_sb"], e.n())
                for k in range(3):
                    w = P if k < 2 else IB
                    ins = te.transpose(bank[3][0:w, k * P:(k + 1) * P], he[:, e.b, k * P:k * P + w], ident[:, :])
                ins.then_inc(e_["hT_ps"], 1)

            def second(e):
                pe.wait_ge(e_["hT_sb"], e.n(1))
                pe.wait_ge(w2_in[e.b], e.dma())
                pe.wait_ge(w2r_in[e.b], e.dma())
                if e.past(1):
                    pe.wait_ge(e_["y_sb"], e.n())
                for k in range(3):
                    w = P if k < 2 else IB
                    ins = te.matmul(bank[4][:, :], heT[0:w, k, :], w2_sb[0:w, e.b, k, :], start=k == 0, stop=k == 2)
                ins.then_inc(e_["y_ps"], 1)

            slot_table(At(0, 0))
            slot_table(At(0, 1))
            xe_T(At(0, 0))

            def phase_b(at):
                if at.cur:
                    first(at.cur)
                if at.prev:
                    he_T(at.prev)
                if at.next:
                    xe_T(at.next)
                if at.after:
                    slot_table(at.after)
                if at.prev:
                    second(at.prev)

            turns(pe, NE, phase_b, 3)

            pe.wait_ge(e_["y_sb"], NE)
            pe.wait_ge(w_att_in, 48)
            W_OG, W_IG, W_O = range(3)

            def attT_ps(t):
                pe.wait_ge(c["gT_sb"], t.n(1))
                if t.past(1):
                    pe.wait_ge(c["at_sb"], t.n())
                te.matmul(bank[0][:, 0:P], att_l[0:DK, 1, :], att_l[0:DK, 0, :], start=True, stop=True
                          ).then_inc(c["at_ps"], 1)

            def state_add(t):
                pe.wait_ge(v_in[t.b], t.dma())
                pe.wait_ge(c["nat_done"], t.n(1))
                if t.past(1):
                    pe.wait_ge(c["s_next"], t.n())
                te.matmul(bank[1][0:2 * DK, :], qk_c[:, 1, :, :].rearrange("p c k -> p (c k)"), v_t[:, t.b, :],
                          start=True, stop=True).then_inc(c["ds_ps"], 1)

            def gate_in(t):
                pe.wait_ge(c["vT_sb"], t.n(1))
                if t.past(1):
                    pe.wait_ge(c["sil_done"], t.n())
                chunks(bank[4][:, :], lambda k: vT[:, k, :], lambda k: w_att[:, W_IG, k, :], DC, True, False
                       ).then_inc(c["wig_ps"], 1)

            def gate_o(t):
                pe.wait_ge(c["oT_sb"], t.n(1))
                chunks(bank[4][:, :], lambda k: oT[:, k, :], lambda k: w_att[:, W_OG, k, :], DC, False, True
                       ).then_inc(c["go_ps"], 1)

            def cumulate(t):
                pe.wait_ge(c["gf_done"], t.n(1))
                if t.past(1):
                    pe.wait_ge(c["vT_sb"], t.n())
                for k, m in enumerate((from_mid, causal, to_last, same_chunk)):
                    ins = te.matmul(bank[5][:, k * DK:(k + 1) * DK], m[:, :], gfn, start=True, stop=True)
                ins.then_inc(c["cum_ps"], 1)

            def output(t):
                pe.wait_ge(c["at_sb"], t.n(1))
                pe.wait_ge(c["s_mid"], t.n(1))
                if t.past(1):
                    pe.wait_ge(c["o_sb"], t.n())
                te.matmul(bank[2][:, :], attT, v_t[:, t.b, :], start=True, stop=False)
                te.matmul(bank[2][:, :], att_l[0:2 * DK, 2, :], state[0:2 * DK, t.b, :], start=False, stop=True
                          ).then_inc(c["o_ps"], 1)

            def o_T(t):
                pe.wait_ge(c["o_sb"], t.n(1))
                if t.past(1):
                    pe.wait_ge(c["ogT_sb"], t.n())
                transposes(3, o_sb).then_inc(c["oT_ps"], 1)

            def og_T(t):
                pe.wait_ge(c["og_done"], t.n(1))
                pe.wait_ge(c["oT_sb"], t.n(1))
                transposes(3, og).then_inc(c["ogT_ps"], 1)

            def out_product(t):
                pe.wait_ge(c["ogT_sb"], t.n(1))
                if t.past(1):
                    pe.wait_ge(c["res_done"], t.n())
                chunks(bank[7][:, :], lambda k: ogT[:, k, :], lambda k: w_att[:, W_O, k, :], DC
                       ).then_inc(c["out_ps"], 1)

            def decayed_T(t):
                pe.wait_ge(c["nat_done"], t.n(1))
                if t.past(1):
                    pe.wait_ge(c["gT_sb"], t.n())
                te.transpose(bank[6][0:DK, 0:P], q_mid, ident[:, :])
                te.transpose(bank[6][0:DK, P:2 * P], k_mid, ident[:, :])
                te.transpose(bank[6][0:2 * DK, 2 * P:3 * P], qk_c[:, 0, :, :].rearrange("p c k -> p (c k)"),
                             ident[:, :])
                te.transpose(bank[6][0:2 * DK, 3 * P:4 * P], decay.rearrange("p c k -> p (c k)"), ident[:, :]
                             ).then_inc(c["gT_ps"], 1)

            def v_T(t):
                pe.wait_ge(v_in[t.b], t.dma())
                pe.wait_ge(c["exm_done"], t.n(1))
                transposes(5, v_t[:, t.b, :]).then_inc(c["vT_ps"], 1)

            cumulate(At(0, 0))
            decayed_T(At(0, 0))
            v_T(At(0, 0))

            def phase_c(at):
                if at.cur:
                    attT_ps(at.cur)
                    state_add(at.cur)
                    gate_in(at.cur)
                if at.next:
                    cumulate(at.next)
                if at.prev:
                    og_T(at.prev)
                if at.cur:
                    output(at.cur)
                if at.prev:
                    out_product(at.prev)
                if at.cur:
                    o_T(at.cur)
                if at.next:
                    decayed_T(at.next)
                if at.cur:
                    gate_o(at.cur)
                if at.next:
                    v_T(at.next)

            turns(pe, NT, phase_c, 1)


def kernel(**inputs):
    import numpy as np
    import concourse.bacc as bacc
    from concourse.bass_utils import run_bass_kernel_spmd

    P = 128

    def rows_first(w):
        return np.ascontiguousarray(w.reshape(-1, P, w.shape[-1]).transpose(1, 0, 2))

    g = {k: np.asarray(a) for k, a in inputs.items()}
    x = g["L0_attn_x"]
    w13 = np.concatenate([g["L1_ffn_w1"], g["L1_ffn_w3"]], 1)
    w13 = w13.transpose(0, 2, 1).reshape(w13.shape[0], -1, P, w13.shape[1]).transpose(0, 2, 1, 3)
    w2 = g["L1_ffn_w2"].transpose(0, 2, 1)
    w2a = w2[:, :2 * P].reshape(w2.shape[0], 2, P, -1).transpose(0, 2, 1, 3)
    arrays = {
        "x": x.reshape(x.shape[1:]),
        "w_ffn": g["L0_ffn_weight"],
        "b_ffn": g["L0_ffn_bias"],
        "w_rqk": rows_first(np.concatenate([g["L1_ffn_gate_w"], g["L1_attn_Wq"], g["L1_attn_Wk"]], 0).T),
        "w_og": rows_first(g["L1_attn_Wog"].T),
        "w_ig": rows_first(g["L1_attn_Wig"].T),
        "w_o": rows_first(g["L1_attn_Wo"].T),
        "g_norm": g["L1_attn_g_norm_w"].reshape(-1, P).T,
        "w_sh13": rows_first(np.concatenate([g["L1_ffn_sw1"], g["L1_ffn_sw3"]], 0).T),
        "w_sh2": g["L1_ffn_sw2"].T,
        "w13": w13,
        "w2a": w2a,
        "w2b": w2[:, 2 * P:],
    }
    arrays = {k: np.ascontiguousarray(v) for k, v in arrays.items()}
    nc = bacc.Bacc("TRN2", target_bir_lowering=False, num_devices=1)
    f32 = mybir.dt.float32
    args = [nc.dram_tensor("in_" + k, v.shape, f32, kind="ExternalInput").ap() for k, v in arrays.items()]
    out = nc.dram_tensor("out", arrays["x"].shape, f32, kind="ExternalOutput").ap()
    xn_rows = nc.dram_tensor("xn_rows", arrays["x"].shape, f32, kind="Internal").ap()
    ye_rows = nc.dram_tensor("ye_rows", (w13.shape[0] * P, x.shape[2]), f32, kind="Internal").ap()
    two_layers(nc, *args, out, xn_rows, ye_rows)
    r = run_bass_kernel_spmd(nc, [{"in_" + k: v for k, v in arrays.items()}], core_ids=[0])
    return r.results[0]["out"].reshape(x.shape)
```

```python
import concourse.bass as bass
from concourse import mybir
from contextlib import ExitStack


class At:

    def __init__(self, i, off):
        self.i, self.off, self.b = i, off, off % 2

    def n(self, add=0):
        return self.i * 2 + (self.off + add)

    def dma(self, back=0):
        return self.i * 16 + 16 * (self.off // 2 + 1 - back)

    def dma2(self):
        return self.i * 32 + 32 * (self.off // 2 + 1)

    def past(self, k):
        return not isinstance(self.i, int) or self.off >= k

    def plus(self, k):
        return At(self.i, self.off + k)


class Turn:

    def __init__(self, at, count):
        static = isinstance(at.i, int)
        self.prev = at.plus(-1) if at.off >= 1 else None
        self.cur = at if not static or at.off < count else None
        self.next = at.plus(1) if not static or at.off + 1 < count else None
        self.after = at.plus(2) if not static or at.off + 2 < count else None


def turns(engine, count, turn, tail):
    for k in range(3):
        turn(Turn(At(0, k), count))
    with engine.Fori(0, (count - 3 - tail) // 2) as i:
        turn(Turn(At(i, 3), count))
        turn(Turn(At(i, 4), count))
    for k in range(count - tail, count + 1):
        turn(Turn(At(0, k), count))


def two_layers(nc, x, w_ffn, b_ffn, w_rqk, w_og, w_ig, w_o, g_norm, w_sh13, w_sh2, w13, w2a, w2b, out,
               xn_rows, ye_rows, slot_token):
    f32, f32r, bf16, u32 = mybir.dt.float32, mybir.dt.float32r, mybir.dt.bfloat16, mybir.dt.uint32
    ALU, ACT, AX = mybir.AluOpType, mybir.ActivationFunctionType, mybir.AxisListType

    P = 128
    N, D = x.shape
    NT = N // P
    DC = D // P
    H, HD = 16, 32
    HP = H // 2
    SEGQ = P // 2
    NE, TOPK, CAP = w13.shape[0], 6, 128
    I2 = w13.shape[3]
    IE = I2 // 2
    IA, IB = 2 * P, IE - 2 * P
    SI = w_sh13.shape[2] // 2
    SQ = SI // 2
    SC = -(-SI // P)
    SR = SI - (SC - 1) * P
    DK = 32
    ATT_SCALE = float(HD) ** -0.5
    EPS = 1e-5
    MAGIC = 12582912.0
    QMAX = 127.0

    x_tiles = x.rearrange("(t j r) d -> t r j d", r=2, j=SEGQ)
    out_tiles = out.rearrange("(t j r) d -> t r j d", r=2, j=SEGQ)
    xn_tiles = xn_rows.rearrange("(t p) d -> t p d", p=P)
    listed = slot_token[0:NE * CAP, :].rearrange("(e s) o -> e (s o)", s=CAP)
    ye_tiles = ye_rows.rearrange("(e p) d -> e p d", p=CAP)

    ctx = ExitStack()
    with ctx:
        def sb(name, shape, dt=f32):
            return ctx.enter_context(nc.sbuf_tensor(name, shape, dt))

        def pb(name, shape, dt=f32):
            return ctx.enter_context(nc.psum_tensor(name, shape, dt))

        def sem(name):
            return ctx.enter_context(nc.semaphore(name))

        ident = sb("ident", [P, P])
        ident_bf = sb("ident_bf", [P, P], bf16)
        ones_mat = sb("ones_mat", [P, P])
        ones_bf = sb("ones_bf", [P, P], bf16)
        slot_row = sb("slot_row", [P, P])
        token_row = sb("token_row", [P, P])
        part_col = sb("part_col", [P, 1])
        token_col = sb("token_col", [P, 1])
        chunk_row = sb("chunk_row", [P, P])
        chunk_col = sb("chunk_col", [P, 1])
        tmp_col = sb("tmp_col", [P, 4])
        same_chunk = sb("same_chunk", [P, P])
        causal = sb("causal", [P, P])
        first_half = sb("first_half", [P, P])
        from_mid = sb("from_mid", [P, P])
        to_last = sb("to_last", [P, P])
        before_bf = sb("before_bf", [P, P], bf16)
        head_rows = sb("head_rows", [P, 2 * DC, 2])
        head_want = sb("head_want", [P, 2 * DC, 2])
        chunk_of = sb("chunk_of", [P, 2])
        token_no = sb("token_no", [P, NT])
        spare = sb("spare", [P, NT, TOPK])
        gnorm = sb("gnorm", [P, DC])
        wqT = sb("wqT", [P, DC, D], bf16)

        W13, W2 = DC * I2, 3 * D
        WE = W13 + W2
        S13, S2 = DC * 2 * SI, SC * D
        assert S13 + S2 <= 2 * WE and 2 * DC * D <= WE
        raw = sb("raw", [P, 2, WE])
        w_hi = sb("w_hi", [P, 2, WE], f32r)
        w_lo = sb("w_lo", [P, 2, WE], f32r)
        wr_hi = sb("wr_hi", [P, DC, P], f32r)
        wr_lo = sb("wr_lo", [P, DC, P], f32r)
        a_hi = sb("a_hi", [P, 3 * D], f32r)
        a_lo = sb("a_lo", [P, 3 * D], f32r)

        def both(view):
            return view(w_hi), view(w_lo)

        def flat(w):
            return w[:, :, :].rearrange("p b i -> p (b i)")

        def acts(at, chunks):
            return tuple(w[:, at:at + chunks * P].rearrange("p (c k) -> p c k", c=chunks) for w in (a_hi, a_lo))

        sh13 = both(lambda w: flat(w)[:, 0:S13].rearrange("p (c i) -> p c i", c=DC))
        sh2 = both(lambda w: flat(w)[:, S13:S13 + S2].rearrange("p (c d) -> p c d", c=SC))
        e13 = both(lambda w: w[:, :, 0:W13].rearrange("p b (c i) -> p b c i", c=DC))
        e2 = both(lambda w: w[:, :, W13:WE].rearrange("p b (c d) -> p b c d", c=3))
        w_og2, w_ig2, w_o2 = (both(lambda w: w[:, b, m * DC * D:(m + 1) * DC * D].rearrange(
            "p (c d) -> p c d", c=DC)) for b, m in ((1, 0), (0, 0), (0, 1)))
        xn2T, hsT = acts(0, DC), acts(D, SC)
        xeT, heT = (acts(0, DC), acts(D, DC)), acts(2 * D, 3)
        vT, oT, ogT = acts(0, DC), acts(D, DC), acts(2 * D, DC)

        acc = sb("acc", [P, NT, D])
        qk_logits = sb("qk_logits", [P, NT, 2 * DK])
        gates = sb("gates", [P, NT, TOPK])
        rows_of = sb("rows_of", [P, NT, TOPK], u32)
        token_now = sb("token_now", [P, 2, 1])
        list_at = sb("list_at", [P, 2, TOPK], u32)

        WORK = 9216
        work = sb("work", [P, WORK])
        used = [0]

        def carve(space, size_of_space, shape):
            size = 1
            for s in shape:
                size *= s
            v = space[:, used[0]:used[0] + size]
            used[0] += size
            assert used[0] <= size_of_space
            if len(shape) == 1:
                return v
            names = "abcd"[:len(shape)]
            return v.rearrange(f"p ({' '.join(names)}) -> p {' '.join(names)}",
                               **{k: s for k, s in zip(names[:-1], shape[:-1])})

        def wk(*shape):
            return carve(work, WORK, shape)

        wn = acc[:, 0:DC, :]
        wdiag = acc[:, DC, :].rearrange("p (c k) -> p c k", c=DC)
        wrqk = acc[:, DC + 1, :].rearrange("p (c k) -> p c k", c=DC)
        wq = acc[:, DC + 2:DC + 4, :].rearrange("p a d -> p (a d)").bitcast(bf16).rearrange(
            "p (c d) -> p c d", c=DC)
        wcols = sb("wcols", [P, 3, DC])
        bias_bc = wk(D)
        wscale_bc = wk(D)
        xin = wk(2, D)
        xn = wk(2, D)
        x_bias = wk(2, D)
        xnT = wk(DC, P)
        xn_heads = wk(2 * DC, 2, SEGQ)
        dist = wk(HP, SEGQ)
        eT = wk(HP, P)
        probs = wk(HP, P)
        y = wk(D)
        xq_f = dist.rearrange("p h j -> p (h j)")
        att = wk(HP, 2, HD)
        used[0] = 0
        x1 = carve(raw[:, 1, :], WE, (2, D))
        xn2 = carve(raw[:, 1, :], WE, (2, D))
        hs = carve(raw[:, 1, :], WE, (SI,))
        chosen = carve(raw[:, 1, :], WE, (TOPK, NE))
        chosen_pos = carve(raw[:, 1, :], WE, (TOPK, NE))
        xq = sb("xq", [P, D], bf16)
        xqT = sb("xqT", [P, DC, P], bf16)
        stats = sb("stats", [P, 2, 6])
        mv = sb("mv", [P, 2, 2])
        rstd = sb("rstd", [P, 2, 1])
        epow = sb("epow", [P, 1])
        xmax = sb("xmax", [P, 1])
        xscale = sb("xscale", [P, 2, 1])
        xinv = sb("xinv", [P, 1])
        smax = sb("smax", [P, HP])
        esum = sb("esum", [P, HP])
        einv = sb("einv", [P, HP])
        gmax = sb("gmax", [P, 1])
        glog = sb("glog", [P, NE])
        gexp = sb("gexp", [P, NE])
        gsum = sb("gsum", [P, 1])
        ginv = sb("ginv", [P, 1])
        score = sb("score", [P, NE])
        top_v = sb("top_v", [P, 8])
        top_i = sb("top_i", [P, 8], u32)
        top_f = sb("top_f", [P, 8])
        mask_bf = sb("mask_bf", [P, NE], bf16)
        msum_bf = sb("msum_bf", [P, NE], bf16)
        pos_k = sb("pos_k", [P, TOPK])
        pos_c = sb("pos_c", [P, TOPK])
        keep = sb("keep", [P, TOPK])
        dropped = sb("dropped", [P, TOPK])
        row_of = sb("row_of", [P, TOPK])
        used[0] = 0
        lists = sb("lists", [P, CAP])
        row_i = sb("row_i", [P, NE], u32)
        row_now = sb("row_now", [P, 2, 1], u32)
        xe = wk(2, D)
        hsil = wk(IE)
        he = wk(2, IE)
        ye = wk(2, D)
        qk_all = wk(2, NT, DK)
        q_all, k_all = qk_all[:, 0, :, :], qk_all[:, 1, :, :]
        ex = wk(4, NT, DK)
        exm = wk(NT, DK)
        k_log, k_exp, q_dist, k_gate = (ex[:, m, :, :] for m in range(4))
        gfn = exm
        v_t = wk(2, D)
        attT = wk(P)
        att_l = wk(4, P)
        q_mid, k_mid = wk(DK), wk(DK)
        decay = wk(2, DK)
        qk_e = wk(2, DK)
        qk_c = wk(2, 2, DK)
        osq, orstd = wk(1), wk(1)
        o_sb = wk(D)
        q_max, q_sum = sb("q_max", [P, NT]), sb("q_sum", [P, NT])
        used[0] = 0
        state = wk(2, D)
        sil = wk(D)
        og = wk(D)
        racc = wk(2, D)

        gat = raw[:, 1, 0:TOPK * D].rearrange("p (k d) -> p k d", k=TOPK)
        res = raw[:, 0, 0:2 * D].rearrange("p (b d) -> p b d", b=2)
        row_k = sb("row_k", [P, 2, TOPK], u32)

        bank = [pb(f"bank{i}", [P, 512]) for i in range(8)]
        cum_ps = [bank[b][:, :] for b in (6, 7, 3, 4)]

        def split4(b):
            return b[:, :].rearrange("p (c k) -> p c k", c=4)

        s_wn, s_c0 = sem("s_wn"), sem("s_c0")
        s_iota, s_const, s_set = sem("s_iota"), sem("s_const"), sem("s_set")
        s_wq, s_wqT, s_wqe, s_zero = sem("s_wq"), sem("s_wqT"), sem("s_wqe"), sem("s_zero")
        s_wsh, s_wsh2, s_wr_hi, s_wr_lo = sem("s_wsh"), sem("s_wsh2"), sem("s_wr_hi"), sem("s_wr_lo")
        s_sh_hi, s_sh_lo = sem("s_sh_hi"), sem("s_sh_lo")
        s_apart = sem("s_apart")
        x_in = [sem("x_in0"), sem("x_in1")]
        names = ("stat1 var1 rstd1 ln_steps xn_done xq_done xb_done xnT_ps xqT_ps xnT_sb xqT_sb xnh_done s_ps "
                 "smax_done dist_done exp_done esum_done f_ps y_scaled y_done eT_ps0 eT_ps1 eT_sb att_ps sum_steps x1_done stat2 var2 "
                 "rstd2 xn2_done xn2T_ps xn2T_hi xn2T_lo lg_ps lg_sb gmax_done gexp_done rt_steps mask_done pos_ps "
                 "slot_steps wa_ps wb_ps wc_ps wd_ps silA silB hA_done hB_done hT_ps hT_hi hT_lo z_ps acc_done")
        a = {k: sem("a_" + k) for k in names.split()}
        xn_out = [sem("xn_out0"), sem("xn_out1")]
        listed_in = [sem("listed_in0"), sem("listed_in1")]
        s_lists, s_listT, s_rows = sem("s_lists"), sem("s_listT"), sem("s_rows")
        w13_in = [sem("w13_in0"), sem("w13_in1")]
        w2_in = [sem("w2_in0"), sem("w2_in1")]
        xe_in = [sem("xe_in0"), sem("xe_in1")]
        ye_out = [sem("ye_out0"), sem("ye_out1")]
        names = ("row_now w13_hi w13_lo w2_hi w2_lo w2_lo2 xeT_ps xeT_hi xeT_lo h1_ps h3_ps sil_done h_done hT_ps "
                 "hT_hi hT_lo y_ps y_sb")
        e_ = {k: sem("b_" + k) for k in names.split()}
        w_gate_in, w_gate_in2, w_o_in, w_o_scaled = sem("w_gate_in"), sem("w_gate_in2"), sem("w_o_in"), sem("w_o_scaled")
        g_steps, g_exp, g_ln, g_cum, g_decays = (
            sem("g_steps"), sem("g_exp"), sem("g_ln"), sem("g_cum"), sem("g_decays"))
        w_att_hi, w_att_lo = sem("w_att_hi"), sem("w_att_lo")
        v_in = [sem("v_in0"), sem("v_in1")]
        gat_in = [sem(f"gat_in{k}") for k in range(TOPK)]
        res_out = [sem("res_out0"), sem("res_out1")]
        names = ("nat_done gT_ps gT_sb vT_ps vT_hi vT_lo at_ps at_sb ds_ps qk_e s_mid s_next wig_ps o_ps o_sb "
                 "sq_done ms_done rstd oT_ps oT_hi oT_lo go_ps sil_done og_done ogT_ps ogT_hi ogT_lo out_ps res_done "
                 "gat_used row_k")
        c = {k: sem("c_" + k) for k in names.split()}

        block = ctx.enter_context(nc.Block())

        @block.sync
        def _(sp):
            def load_x(t):
                for r in range(2):
                    sp.dma_start(xin[r * SEGQ:(r + 1) * SEGQ, t.b, :],
                                 x_tiles[bass.ds(t.n(), 1), r, :, :].rearrange("o j d -> (o j) d")
                                 ).then_inc(x_in[t.b], 16)

            load_x(At(0, 0))
            sp.wait_ge(s_zero, 1)
            sp.dma_start(listed, lists[0:NE, :]).then_inc(s_lists, 16)
            sp.dma_start(wn, w_ffn.rearrange("(c p) d -> p c d", p=P)).then_inc(s_wn, 16)
            sp.dma_start(bias_bc[:, :], b_ffn.partition_broadcast(P)).then_inc(s_c0, 16)
            sp.dma_start(gnorm[:, :], g_norm).then_inc(s_c0, 16)
            sp.dma_start(wrqk, w_rqk).then_inc(s_c0, 16)
            load_x(At(0, 1))
            flat_raw = flat(raw)
            sp.dma_start(flat_raw[:, 0:S13].rearrange("p (c i) -> p c i", c=DC), w_sh13).then_inc(s_wsh, 16)
            sp.dma_start(flat_raw[:, S13:S13 + S2 - D].rearrange("p (c d) -> p c d", c=SC - 1),
                         w_sh2[0:(SC - 1) * P, :].rearrange("(c p) d -> p c d", p=P)).then_inc(s_wsh2, 16)
            sp.dma_start(flat_raw[0:SR, S13 + S2 - D:S13 + S2], w_sh2[(SC - 1) * P:SI, :]).then_inc(s_wsh2, 16)

            def load_w13(e):
                sp.dma_start(raw[:, e.b, 0:W13].rearrange("p (c i) -> p c i", c=DC),
                             w13[bass.ds(e.n(), 1), :, :, :].rearrange("o p c i -> (o p) c i")
                             ).then_inc(w13_in[e.b], 16)

            def load_w2(e):
                sp.dma_start(raw[:, e.b, W13:WE - D].rearrange("p (c d) -> p c d", c=2),
                             w2a[bass.ds(e.n(), 1), :, :, :].rearrange("o p c d -> (o p) c d")
                             ).then_inc(w2_in[e.b], 16)
                sp.dma_start(raw[0:IB, e.b, WE - D:WE],
                             w2b[bass.ds(e.n(), 1), :, :].rearrange("o p d -> (o p) d")
                             ).then_inc(w2_in[e.b], 16)

            def phase_a(t):
                sp.wait_ge(a["xn2_done"], t.n(1))
                sp.dma_start(xn_tiles[bass.ds(t.n(), 1), :, :].rearrange("o p d -> (o p) d"),
                             xn2[:, t.b, :]).then_inc(xn_out[t.b], 16)

            for t in (0,):
                sp.wait_ge(s_sh_lo, 2)
                load_w13(At(0, 0))
                load_w2(At(0, 0))
                sp.wait_ge(a["xb_done"], 1)
                sp.wait_ge(a["xn_done"], 1)
                load_x(At(0, 2))
                phase_a(At(0, 0))
            with sp.Fori(0, (NT - 4) // 2) as i:
                for off in (1, 2):
                    t = At(i, off)
                    sp.wait_ge(a["xb_done"], t.n(1))
                    sp.wait_ge(a["xn_done"], t.n(1))
                    load_x(t.plus(2))
                    phase_a(t)
            sp.wait_ge(a["xb_done"], NT - 2)
            sp.wait_ge(a["xn_done"], NT - 2)
            load_x(At(0, NT - 1))
            for t in (NT - 3, NT - 2, NT - 1):
                phase_a(At(0, t))

            sp.wait_ge(a["acc_done"], NT)
            for b in range(2):
                sp.wait_ge(xn_out[b], 16 * (NT // 2))
            load_w13(At(0, 1))
            load_w2(At(0, 1))
            for b in range(2):
                sp.wait_ge(listed_in[b], 16 * TOPK * (NT // 2))
            sp.dma_start(lists[0:NE, :], listed).then_inc(s_lists, 16)


            def store(e):
                sp.wait_ge(e_["y_sb"], e.n(1))
                sp.dma_start(ye_tiles[bass.ds(e.n(), 1), :, :].rearrange("o p d -> (o p) d"),
                             ye[:, e.b, :]).then_inc(ye_out[e.b], 16)

            def ahead13(e):
                sp.wait_ge(e_["w13_lo"], e.n(1))
                load_w13(e.plus(2))

            def ahead2(e):
                sp.wait_ge(e_["w2_lo"], e.n(1))
                sp.wait_ge(e_["w2_lo2"], e.n(1))
                load_w2(e.plus(2))

            ahead13(At(0, 0))
            ahead13(At(0, 1))
            with sp.Fori(0, (NE - 4) // 2) as i:
                for off in (1, 2):
                    e = At(i, off)
                    ahead13(e.plus(1))
                    ahead2(e.plus(-1))
                    store(e.plus(-1))
            ahead2(At(0, NE - 4))
            sp.wait_ge(e_["w13_lo"], NE)
            for b, (w, done) in enumerate(((w_ig, w_gate_in), (w_og, w_gate_in2))):
                sp.dma_start(raw[:, b, 0:DC * D].rearrange("p (c d) -> p c d", c=DC), w).then_inc(done, 16)
            store(At(0, NE - 4))
            ahead2(At(0, NE - 3))
            store(At(0, NE - 3))
            sp.wait_ge(e_["w2_lo"], NE - 1)
            sp.wait_ge(e_["w2_lo2"], NE - 1)
            sp.dma_start(raw[:, 0, DC * D:2 * DC * D].rearrange("p (c d) -> p c d", c=DC), w_o).then_inc(w_o_in, 16)
            for e in (NE - 2, NE - 1):
                store(At(0, e))

            def load_v(t):
                sp.dma_start(v_t[:, t.b, :],
                             xn_tiles[bass.ds(t.n(), 1), :, :].rearrange("o p d -> (o p) d")
                             ).then_inc(v_in[t.b], 16)

            def store_res(t):
                sp.wait_ge(c["res_done"], t.n(1))
                for r in range(2):
                    sp.dma_start(out_tiles[bass.ds(t.n(), 1), r, :, :].rearrange("o j d -> (o j) d"),
                                 res[r * SEGQ:(r + 1) * SEGQ, t.b, :]).then_inc(res_out[t.b], 16)

            load_v(At(0, 0))
            load_v(At(0, 1))
            sp.wait_ge(c["o_ps"], 1)
            sp.wait_ge(c["vT_ps"], 1)
            load_v(At(0, 2))
            with sp.Fori(0, (NT - 4) // 2) as i:
                for off in (1, 2):
                    t = At(i, off)
                    sp.wait_ge(c["o_ps"], t.n(1))
                    load_v(t.plus(2))
                    store_res(t.plus(-1))
            sp.wait_ge(c["o_ps"], NT - 2)
            load_v(At(0, NT - 1))
            for t in (NT - 4, NT - 3, NT - 2, NT - 1):
                store_res(At(0, t))
            for b in range(2):
                sp.wait_ge(res_out[b], 16 * NT)

        @block.gpsimd
        def _(pool):
            nc.gpsimd.memset(lists[:, :], 0.0).then_inc(s_zero, 1)
            nc.gpsimd.iota(slot_row[:, :], [[1, P]], base=0, channel_multiplier=0,
                           allow_small_or_imprecise_dtypes=True).then_inc(s_iota, 1)
            nc.gpsimd.iota(token_row[:, :], [[1, 2], [2, SEGQ]], base=0, channel_multiplier=0,
                           allow_small_or_imprecise_dtypes=True).then_inc(s_iota, 1)
            nc.gpsimd.iota(part_col[:, :], [[1, 1]], base=0, channel_multiplier=1,
                           allow_small_or_imprecise_dtypes=True).then_inc(s_iota, 1)
            nc.gpsimd.iota(head_want[:, :, :], [[0, DC], [1, 2], [2, 2]], base=0, channel_multiplier=0,
                           allow_small_or_imprecise_dtypes=True).then_inc(s_iota, 1)
            nc.gpsimd.iota(token_no[:, :], [[P, NT]], base=0, channel_multiplier=1,
                           allow_small_or_imprecise_dtypes=True).then_inc(s_iota, 1)
            nc.gpsimd.iota(spare[:, :, :], [[TOPK * P, NT], [P, TOPK]], base=NE * CAP, channel_multiplier=1,
                           allow_small_or_imprecise_dtypes=True).then_inc(s_iota, 1)
            nc.gpsimd.memset(epow[:, :], -0.5).then_inc(s_zero, 1)
            nc.gpsimd.memset(ones_mat[:, :], 1.0).then_inc(s_zero, 1)
            nc.gpsimd.memset(ones_bf[:, :], 1.0).then_inc(s_zero, 1)
            nc.gpsimd.memset(probs[:, :, :], 0.0).then_inc(s_zero, 1)
            nc.gpsimd.memset(msum_bf[:, :], 0.0).then_inc(s_zero, 1)

            def rsqrt(which, ready, added, done, t):
                pool.wait_ge(ready, t.n(1))
                plain()
                nc.gpsimd.tensor_scalar(rstd[:, which, :], mv[:, which, 1:2], EPS, None, ALU.add
                                        ).then_inc(added, 1)
                pool.wait_ge(added, t.n(1))
                nc.gpsimd.tensor_tensor(rstd[:, which, :], rstd[:, which, :], epow[:, :], ALU.pow
                                        ).then_inc(done, 1)

            def plain():
                pool.sem_inc(s_apart, 1)

            pool.wait_ge(s_zero, 6)
            pool.wait_ge(s_c0, 48)

            def norm1(t):
                pool.wait_ge(x_in[t.b], t.dma2())
                nc.gpsimd.tensor_tensor(x_bias[:, t.b, :], xin[:, t.b, :], bias_bc[:, :], ALU.add
                                        ).then_inc(a["xb_done"], 1)
                rsqrt(0, a["stat1"], a["var1"], a["rstd1"], t)

            def norm2(t):
                rsqrt(1, a["stat2"], a["var2"], a["rstd2"], t)

            def enlist(t):
                pool.wait_ge(a["slot_steps"], t.n(1) * 7)
                for k in range(TOPK):
                    plain()
                    nc.gpsimd.indirect_dma_start(
                        slot_token[:, :],
                        bass.IndirectOffsetOnAxis(ap=list_at[:, t.b, k:k + 1], axis=0),
                        token_now[:, t.b, :], None).then_inc(listed_in[t.b], 16)

            def spread_heads(t):
                pool.wait_ge(a["xnT_sb"], t.n(1))
                if t.past(1):
                    pool.wait_ge(a["s_ps"], t.n())
                src = xnT.rearrange("p c (r o j) -> p (c r) o j", r=2, o=1)
                nc.gpsimd.tensor_tensor(xn_heads, src.to_broadcast([P, 2 * DC, 2, SEGQ]),
                                        head_rows[:, :, :].unsqueeze(3).to_broadcast([P, 2 * DC, 2, SEGQ]),
                                        ALU.mult).then_inc(a["xnh_done"], 1)

            def split_shared():
                pool.wait_ge(s_sh_hi, 3)
                w = flat(w_lo)
                nc.gpsimd.tensor_tensor(w[:, S13:S13 + S2 - D], flat(raw)[:, S13:S13 + S2 - D],
                                        flat(w_hi)[:, S13:S13 + S2 - D].bitcast(f32), ALU.subtract)
                nc.gpsimd.tensor_tensor(w[0:SR, S13 + S2 - D:S13 + S2], flat(raw)[0:SR, S13 + S2 - D:S13 + S2],
                                        flat(w_hi)[0:SR, S13 + S2 - D:S13 + S2].bitcast(f32), ALU.subtract
                                        ).then_inc(s_sh_lo, 1)

            norm1(At(0, 0))
            pool.wait_ge(s_set, 2)
            spread_heads(At(0, 0))
            split_shared()

            def add_bias(t):
                pool.wait_ge(a["y_scaled"], t.n(1))
                nc.gpsimd.tensor_tensor(y, y, x_bias[:, t.b, :], ALU.add).then_inc(a["y_done"], 1)

            def phase_a(t):
                add_bias(t)
                norm1(t.plus(1))
                if t.past(2):
                    enlist(t.plus(-2))
                norm2(t)
                spread_heads(t.plus(1))

            pool.wait_ge(s_lists, 16)
            pool.wait_ge(s_iota, 6)
            phase_a(At(0, 0))
            phase_a(At(0, 1))
            phase_a(At(0, 2))
            with pool.Fori(0, (NT - 4) // 2) as i:
                phase_a(At(i, 3))
                phase_a(At(i, 4))
            add_bias(At(0, NT - 1))
            enlist(At(0, NT - 3))
            norm2(At(0, NT - 1))
            enlist(At(0, NT - 2))
            enlist(At(0, NT - 1))

            pool.wait_ge(s_rows, 1)
            for b in range(2):
                pool.wait_ge(xn_out[b], 16 * (NT // 2))
            pool.wait_ge(a["acc_done"], NT)

            def gather(e, free):
                if free:
                    pool.wait_ge(xe_in[e.b], e.dma(1))
                nc.gpsimd.tensor_copy(row_now[:, e.b, :], row_i[:, bass.ds(e.n(), 1)]).then_inc(e_["row_now"], 1)
                pool.wait_ge(e_["row_now"], e.n(1))
                if free:
                    pool.wait_ge(e_["xeT_ps"], e.n(-1))
                plain()
                nc.gpsimd.indirect_dma_start(
                    xe[:, e.b, :], None, xn_rows[:, :],
                    bass.IndirectOffsetOnAxis(ap=row_now[:, e.b, :], axis=0)).then_inc(xe_in[e.b], 16)

            def split2_low(e):
                pool.wait_ge(e_["w2_hi"], e.n(1))
                nc.gpsimd.tensor_tensor(w_lo[0:IB, e.b, WE - D:WE], raw[0:IB, e.b, WE - D:WE],
                                        w_hi[0:IB, e.b, WE - D:WE].bitcast(f32), ALU.subtract
                                        ).then_inc(e_["w2_lo2"], 1)

            gather(At(0, 0), False)
            gather(At(0, 1), False)
            with pool.Fori(0, (NE - 2) // 2) as i:
                for off in range(2):
                    gather(At(i, off + 2), True)
                    split2_low(At(i, off))
            split2_low(At(0, NE - 2))
            split2_low(At(0, NE - 1))

            pool.wait_ge(ye_out[0], 16 * (NE // 2))
            pool.wait_ge(ye_out[1], 16 * (NE // 2))
            pool.wait_ge(w_att_lo, 2)

            def gather_rows(t, free):
                for k in range(TOPK):
                    if free:
                        pool.wait_ge(c["gat_used"], (t.n(-1)) * TOPK + (k + 1))
                    plain()
                    nc.gpsimd.indirect_dma_start(
                        gat[:, k, :], None, ye_rows[:, :],
                        bass.IndirectOffsetOnAxis(
                            ap=row_k[:, t.b, k:k + 1], axis=0)
                    ).then_inc(gat_in[k], 16)

            def rsqrt_c(t):
                pool.wait_ge(c["sq_done"], t.n(1))
                if t.past(1):
                    pool.wait_ge(c["og_done"], t.n())
                plain()
                nc.gpsimd.tensor_scalar(orstd, osq, 1.0 / D, EPS, ALU.mult, ALU.add).then_inc(c["ms_done"], 1)
                pool.wait_ge(c["ms_done"], t.n(1))
                nc.gpsimd.tensor_tensor(orstd, orstd, epow[:, :], ALU.pow).then_inc(c["rstd"], 1)

            def copy_rows(t):
                nc.gpsimd.tensor_copy(row_k[:, t.b, :], rows_of[:, bass.ds(t.n(), 1), :]
                                      .rearrange("p o k -> p (o k)")).then_inc(c["row_k"], 1)
                pool.wait_ge(c["row_k"], t.n(1))

            def phase_c(t, free):
                copy_rows(t)
                gather_rows(t, free)
                rsqrt_c(t)

            phase_c(At(0, 0), False)
            phase_c(At(0, 1), True)
            with pool.Fori(0, (NT - 2) // 2) as i:
                phase_c(At(i, 2), True)
                phase_c(At(i, 3), True)

        @block.vector
        def _(dve):
            v = nc.vector
            count = [0]

            def link(ins):
                count[0] += 1
                ins.then_inc(s_const, 1)
                dve.wait_ge(s_const, count[0])

            def plain():
                dve.sem_inc(s_apart, 1)

            class Chain:

                def __init__(self, at, done, k):
                    self.at, self.done, self.k, self.j = at, done, k, 0

                def __call__(self, ins, apart=False):
                    self.j += 1
                    ins.then_inc(self.done, 1)
                    dve.wait_ge(self.done, self.at.n() * self.k + self.j)
                    if apart:
                        plain()

                def end(self):
                    assert self.j == self.k

            v.memset(att, 0.0)
            dve.wait_ge(s_iota, 6)
            v.tensor_scalar(ident[:, :], slot_row[:, :], part_col[:, :], None, ALU.is_equal)
            v.tensor_scalar(ident_bf[:, :], slot_row[:, :], part_col[:, :], None, ALU.is_equal).then_inc(s_set, 1)
            link(v.tensor_scalar(tmp_col[:, 0:1], part_col[:, :], float(SEGQ), -float(P - 1), ALU.is_ge, ALU.mult))
            link(v.scalar_tensor_tensor(token_col[:, :], part_col[:, :], 2.0, tmp_col[:, 0:1], ALU.mult, ALU.add))
            v.tensor_scalar(chunk_of[:, 0:1], token_col[:, :], float(SEGQ), None, ALU.is_lt)
            v.tensor_scalar(chunk_of[:, 1:2], token_col[:, :], float(SEGQ), None, ALU.is_ge)
            link(v.tensor_scalar(chunk_col[:, :], token_col[:, :], float(SEGQ), None, ALU.is_ge))
            link(v.tensor_scalar(chunk_row[:, :], token_row[:, :], float(SEGQ), None, ALU.is_ge))
            v.tensor_scalar(before_bf[:, :], token_row[:, :], token_col[:, :], None, ALU.is_gt)
            link(v.tensor_scalar(same_chunk[:, :], chunk_row[:, :], chunk_col[:, :], None, ALU.is_equal))
            link(v.scalar_tensor_tensor(causal[:, :], token_row[:, :], token_col[:, :], same_chunk[:, :],
                                        ALU.is_ge, ALU.mult))
            link(v.scalar_tensor_tensor(tmp_col[:, 1:2], chunk_col[:, :], -float(SEGQ), token_col[:, :],
                                        ALU.mult, ALU.add))
            link(v.tensor_scalar(tmp_col[:, 2:3], tmp_col[:, 1:2], float(SEGQ // 2), None, ALU.is_lt))
            link(v.tensor_scalar(first_half[:, :], same_chunk[:, :], tmp_col[:, 2:3], None, ALU.mult))
            v.tensor_tensor(from_mid[:, :], causal[:, :], first_half[:, :], ALU.subtract)
            v.tensor_tensor(to_last[:, :], same_chunk[:, :], causal[:, :], ALU.subtract)
            link(v.tensor_scalar(tmp_col[:, 0:1], part_col[:, :], 32.0, None, ALU.is_ge))
            link(v.tensor_scalar(tmp_col[:, 1:2], part_col[:, :], 64.0, None, ALU.is_ge))
            link(v.tensor_scalar(tmp_col[:, 2:3], part_col[:, :], 96.0, None, ALU.is_ge))
            link(v.tensor_tensor(tmp_col[:, 3:4], tmp_col[:, 0:1], tmp_col[:, 1:2], ALU.add))
            link(v.tensor_tensor(tmp_col[:, 0:1], tmp_col[:, 3:4], tmp_col[:, 2:3], ALU.add))
            v.tensor_scalar(head_rows[:, :, :], head_want[:, :, :], tmp_col[:, 0:1], None, ALU.is_equal
                            ).then_inc(s_set, 1)

            def norm1(t, between=None):
                ln = Chain(t, a["ln_steps"], 5)
                dve.wait_ge(x_in[t.b], t.dma2())
                ln(v.bn_stats(stats[:, 0, :], xin[:, t.b, :]), apart=True)
                v.bn_aggr(mv[:, 0, :], stats[:, 0, :]).then_inc(a["stat1"], 1)
                dve.wait_ge(a["rstd1"], t.n(1))
                if t.past(2):
                    dve.wait_ge(a["att_ps"], t.n(-1))
                v.tensor_scalar(xn[:, t.b, :], xin[:, t.b, :], mv[:, 0, 0:1], rstd[:, 0, :],
                                ALU.subtract, ALU.mult).then_inc(a["xn_done"], 1)
                dve.wait_ge(a["xn_done"], t.n(1))
                ln(v.tensor_reduce(xmax[:, :], xn[:, t.b, :], AX.X, ALU.max, apply_absolute_value=True))
                ln(v.tensor_scalar(xscale[:, t.b, :], xmax[:, :], 1.0 / QMAX, 1e-12, ALU.mult, ALU.max))
                ln(v.reciprocal(xinv[:, :], xscale[:, t.b, :]))
                if between:
                    between()
                ln(v.tensor_scalar(xq_f, xn[:, t.b, :], xinv[:, :], MAGIC, ALU.mult, ALU.add))
                if t.past(1):
                    dve.wait_ge(a["xqT_ps"], t.n())
                v.tensor_scalar(xq[:, :], xq_f, MAGIC, None, ALU.subtract).then_inc(a["xq_done"], 1)
                ln.end()

            def xn2T_low(t):
                dve.wait_ge(a["xn2T_hi"], t.n(1))
                v.tensor_tensor(xn2T[1], split4(bank[0]), xn2T[0].bitcast(f32), ALU.subtract
                                ).then_inc(a["xn2T_lo"], 1)

            def hsT_low(t):
                dve.wait_ge(a["hT_hi"], t.n(1))
                v.tensor_tensor(hsT[1][:, 0:4, :], split4(bank[4]), hsT[0][:, 0:4, :].bitcast(f32), ALU.subtract)
                v.tensor_tensor(hsT[1][:, 4, :], bank[5][:, 0:P], hsT[0][:, 4, :].bitcast(f32), ALU.subtract)
                v.tensor_tensor(hsT[1][0:SR, 5, :], bank[5][0:SR, P:2 * P], hsT[0][0:SR, 5, :].bitcast(f32),
                                ALU.subtract).then_inc(a["hT_lo"], 1)

            def split_shared():
                for k in range(2):
                    dve.wait_ge(s_sh_hi, k + 1)
                    part = slice(k * S13 // 2, (k + 1) * S13 // 2)
                    low = v.tensor_tensor(flat(w_lo)[:, part], flat(raw)[:, part],
                                          flat(w_hi)[:, part].bitcast(f32), ALU.subtract)
                low.then_inc(s_sh_lo, 1)

            def router_max(t):
                dve.wait_ge(a["lg_sb"], t.n(1))
                if t.past(1):
                    dve.wait_ge(a["gexp_done"], t.n())
                v.tensor_reduce(gmax[:, :], glog[:, :], AX.X, ALU.max, negate=True
                                ).then_inc(a["gmax_done"], 1)

            def scores(t):
                dve.wait_ge(a["s_ps"], t.n(1))
                s = bank[2][:, :].rearrange("p (h j) -> p h j", h=HP)
                v.tensor_reduce(smax[:, :], s, AX.X, ALU.max).then_inc(a["smax_done"], 1)
                dve.wait_ge(a["smax_done"], t.n(1))
                if t.past(1):
                    dve.wait_ge(a["exp_done"], t.n())
                v.tensor_tensor(dist, s, smax[:, :].unsqueeze(2).to_broadcast([P, HP, SEGQ]), ALU.subtract
                                ).then_inc(a["dist_done"], 1)

            def gate_half(t, half):
                dve.wait_ge(a["silA" if half == 0 else "silB"], t.n(1))
                dve.wait_ge(a["wb_ps" if half == 0 else "wd_ps"], t.n(1))
                part = hs[:, half * SQ:(half + 1) * SQ]
                v.tensor_tensor(part, part, bank[7][:, 0:SQ], ALU.mult
                                ).then_inc(a["hA_done" if half == 0 else "hB_done"], 1)

            def top_experts(t):
                rt = Chain(t, a["rt_steps"], 6)
                dve.wait_ge(a["gexp_done"], t.n(1))
                rt(v.reciprocal(ginv[:, :], gsum[:, :]))
                rt(v.tensor_scalar(score[:, :], gexp[:, :], ginv[:, :], None, ALU.mult), apart=True)
                rt(v.max(top_v[:, :], score[:, :]), apart=True)
                rt(v.max_index(top_i[:, :], top_v[:, :], score[:, :]))
                rt(v.tensor_copy(top_f[:, :], top_i[:, :]))
                rt(v.tensor_tensor(chosen[:, :, :], slot_row[:, 0:NE].unsqueeze(1).to_broadcast([P, TOPK, NE]),
                                   top_f[:, 0:TOPK].unsqueeze(2).to_broadcast([P, TOPK, NE]), ALU.is_equal))
                if t.past(1):
                    dve.wait_ge(a["pos_ps"], t.n())
                with nc.allow_low_precision(reason="zeros and ones"):
                    v.tensor_reduce(mask_bf[:, :], chosen[:, :, :].rearrange("p k e -> p e k"), AX.X, ALU.add
                                    ).then_inc(a["mask_done"], 1)
                rt.end()

            def slots(t):
                sl = Chain(t, a["slot_steps"], 7)
                dve.wait_ge(a["pos_ps"], t.n(1))
                dve.wait_ge(a["mask_done"], t.n(1))
                pos = bank[1][:, 384:384 + NE]
                v.tensor_tensor(msum_bf[:, :], msum_bf[:, :], mask_bf[:, :], ALU.add)
                sl(v.tensor_tensor(chosen_pos[:, :, :], chosen[:, :, :],
                                   pos.unsqueeze(1).to_broadcast([P, TOPK, NE]), ALU.mult))
                sl(v.tensor_reduce(pos_k[:, :], chosen_pos[:, :, :], AX.X, ALU.add))
                v.tensor_scalar(keep[:, :], pos_k[:, :], float(CAP), None, ALU.is_lt)
                v.tensor_scalar(dropped[:, :], pos_k[:, :], float(CAP), None, ALU.is_ge)
                sl(v.tensor_scalar(pos_c[:, :], pos_k[:, :], float(CAP - 1), None, ALU.min))
                v.tensor_tensor(gates[:, bass.ds(t.n(), 1), :].rearrange("p o k -> p (o k)"),
                                top_v[:, 0:TOPK], keep[:, :], ALU.mult)
                sl(v.tensor_tensor(dropped[:, :], dropped[:, :],
                                   spare[:, bass.ds(t.n(), 1), :].rearrange("p o k -> p (o k)"), ALU.mult))
                sl(v.scalar_tensor_tensor(row_of[:, :], top_f[:, 0:TOPK], float(CAP), pos_c[:, :],
                                          ALU.mult, ALU.add))
                sl(v.tensor_copy(rows_of[:, bass.ds(t.n(), 1), :].rearrange("p o k -> p (o k)"), row_of[:, :]))
                if t.past(2):
                    dve.wait_ge(listed_in[t.b], t.i * 16 * TOPK + 16 * TOPK * (t.off // 2))
                v.tensor_copy(token_now[:, t.b, :], token_no[:, bass.ds(t.n(), 1)])
                sl(v.tensor_tensor(list_at[:, t.b, :], row_of[:, :], dropped[:, :], ALU.max))
                sl.end()

            def sums(t):
                dve.wait_ge(a["exp_done"], t.n(1))
                v.tensor_reduce(esum[:, :], probs[:, :, :], AX.X, ALU.add).then_inc(a["esum_done"], 1)
                dve.wait_ge(a["esum_done"], t.n(1))
                v.reciprocal(einv[:, :], esum[:, :])

            def scaled(t):
                dve.wait_ge(a["f_ps"], t.n(1))
                if t.past(1):
                    dve.wait_ge(a["x1_done"], t.n())
                v.scalar_tensor_tensor(y, bank[3][:, :], xscale[:, t.b, :], wscale_bc[:, :], ALU.mult, ALU.mult
                                       ).then_inc(a["y_scaled"], 1)

            def residual(t):
                su = Chain(t, a["sum_steps"], 3)
                dve.wait_ge(a["att_ps"], t.n(1))
                o = bank[2][:, :].rearrange("p (h r d) -> p h r d", h=HP, r=2)
                su(v.tensor_tensor(att[0:SEGQ, :, 0, :], o[0:SEGQ, :, 0, :],
                                   einv[0:SEGQ, :].unsqueeze(2).to_broadcast([SEGQ, HP, HD]), ALU.mult))
                su(v.tensor_tensor(att[SEGQ:P, :, 1, :], o[SEGQ:P, :, 1, :],
                                   einv[SEGQ:P, :].unsqueeze(2).to_broadcast([SEGQ, HP, HD]), ALU.mult))
                dve.wait_ge(a["y_done"], t.n(1))
                v.tensor_tensor(x1[:, t.b, :], y, att.rearrange("p h r d -> p (h r d)"), ALU.add
                                ).then_inc(a["x1_done"], 1)
                dve.wait_ge(a["x1_done"], t.n(1))
                su(v.bn_stats(stats[:, 1, :], x1[:, t.b, :]), apart=True)
                v.bn_aggr(mv[:, 1, :], stats[:, 1, :]).then_inc(a["stat2"], 1)
                su.end()

            def norm2(t):
                dve.wait_ge(a["rstd2"], t.n(1))
                if t.past(2):
                    dve.wait_ge(xn_out[t.b], t.dma(1))
                    dve.wait_ge(a["xn2T_ps"], t.n(-1))
                v.tensor_scalar(xn2[:, t.b, :], x1[:, t.b, :], mv[:, 1, 0:1], rstd[:, 1, :],
                                ALU.subtract, ALU.mult).then_inc(a["xn2_done"], 1)

            def keep_sum(t):
                dve.wait_ge(a["z_ps"], t.n(1))
                v.tensor_tensor(acc[:, bass.ds(t.n(), 1), :].rearrange("p o d -> p (o d)"),
                                x1[:, t.b, :], bank[6][:, :], ALU.add).then_inc(a["acc_done"], 1)

            norm1(At(0, 0))

            dve.wait_ge(s_wn, 16)
            link(v.tensor_reduce(wcols[:, 0, :], wn, AX.X, ALU.max, apply_absolute_value=True))
            link(v.tensor_scalar(wcols[:, 0, :], wcols[:, 0, :], 1e-8, None, ALU.max))
            link(v.tensor_scalar(wcols[:, 1, :], wcols[:, 0, :], 1.0 / QMAX, None, ALU.mult))
            link(v.reciprocal(wcols[:, 2, :], wcols[:, 1, :]))
            for k in range(DC):
                link(v.tensor_scalar(wn[:, k, :], wn[:, k, :], wcols[:, 2, k:k + 1], MAGIC, ALU.mult, ALU.add))
                v.tensor_scalar(wq[:, k, :], wn[:, k, :], MAGIC, None, ALU.subtract).then_inc(s_wq, 1)
                v.tensor_scalar(wdiag[:, k, :], ident[:, :], wcols[:, 1, k:k + 1], None, ALU.mult).then_inc(s_wq, 1)

            def phase_a(at):
                if at.cur:
                    scores(at.cur)
                if at.prev:
                    xn2T_low(at.prev)
                if at.cur:
                    scaled(at.cur)
                    sums(at.cur)
                if at.prev:
                    router_max(at.prev)
                if at.next:
                    norm1(at.next, (lambda: gate_half(at.prev, 0)) if at.prev else None)
                elif at.prev:
                    gate_half(at.prev, 0)
                if at.prev:
                    top_experts(at.prev)
                    gate_half(at.prev, 1)
                else:
                    dve.wait_ge(s_sh_lo, 2)
                if at.cur:
                    residual(at.cur)
                else:
                    slots(at.prev)
                if at.prev:
                    hsT_low(at.prev)
                if at.cur:
                    norm2(at.cur)
                if at.prev:
                    if at.cur:
                        slots(at.prev)
                    keep_sum(at.prev)

            split_shared()
            dve.wait_ge(s_wqe, 2)
            dve.wait_ge(s_wr_hi, 1)
            v.tensor_tensor(wr_lo[:, :, :], wrqk, wr_hi[:, :, :].bitcast(f32), ALU.subtract).then_inc(s_wr_lo, 1)
            dve.wait_ge(s_wr_lo, 1)
            dve.wait_ge(s_zero, 6)
            turns(dve, NT, phase_a, 1)

            def tiles_k(x):
                return x.unsqueeze(2).to_broadcast([P, NT, DK])

            v.tensor_scalar(k_log, qk_logits[:, :, DK:2 * DK], -88.0, None, ALU.max)
            v.tensor_reduce(q_max[:, :], qk_logits[:, :, 0:DK], AX.X, ALU.max).then_inc(g_steps, 1)
            dve.wait_ge(g_steps, 1)
            v.tensor_tensor(q_dist, qk_logits[:, :, 0:DK], tiles_k(q_max[:, :]), ALU.subtract).then_inc(g_steps, 1)
            dve.wait_ge(g_exp, 1)
            v.tensor_reduce(q_sum[:, :], q_dist, AX.X, ALU.add).then_inc(g_steps, 1)
            v.tensor_scalar(k_exp, k_exp, 1.0, None, ALU.add).then_inc(g_steps, 1)
            dve.wait_ge(g_steps, 4)
            v.reciprocal(k_all, k_exp).then_inc(g_steps, 1)
            v.reciprocal(q_sum[:, :], q_sum[:, :]).then_inc(g_steps, 1)
            dve.wait_ge(g_steps, 6)
            v.tensor_tensor(q_all, q_dist, tiles_k(q_sum[:, :]), ALU.mult).then_inc(g_steps, 1)

            def gate_expert(e):
                dve.wait_ge(e_["sil_done"], e.n(1))
                dve.wait_ge(e_["h3_ps"], e.n(1))
                if e.past(2):
                    dve.wait_ge(e_["hT_ps"], e.n(-1))
                v.tensor_tensor(he[:, e.b, :], hsil, bank[1][:, 0:IE], ALU.mult).then_inc(e_["h_done"], 1)

            def split13_low(e):
                dve.wait_ge(e_["w13_hi"], e.n(1))
                v.tensor_tensor(w_lo[:, e.b, 0:W13], raw[:, e.b, 0:W13], w_hi[:, e.b, 0:W13].bitcast(f32),
                                ALU.subtract).then_inc(e_["w13_lo"], 1)

            def split2_low(e):
                dve.wait_ge(e_["w2_hi"], e.n(1))
                v.tensor_tensor(w_lo[:, e.b, W13:WE - D], raw[:, e.b, W13:WE - D],
                                w_hi[:, e.b, W13:WE - D].bitcast(f32), ALU.subtract).then_inc(e_["w2_lo"], 1)

            def xeT_low(e):
                dve.wait_ge(e_["xeT_hi"], e.n(1))
                v.tensor_tensor(xeT[e.b][1], split4(bank[2]), xeT[e.b][0].bitcast(f32), ALU.subtract
                                ).then_inc(e_["xeT_lo"], 1)

            def heT_low(e):
                dve.wait_ge(e_["hT_hi"], e.n(1))
                v.tensor_tensor(heT[1][:, 0:2, :], bank[3][:, 0:2 * P].rearrange("p (c k) -> p c k", c=2),
                                heT[0][:, 0:2, :].bitcast(f32), ALU.subtract)
                v.tensor_tensor(heT[1][0:IB, 2, :], bank[3][0:IB, 2 * P:3 * P], heT[0][0:IB, 2, :].bitcast(f32),
                                ALU.subtract).then_inc(e_["hT_lo"], 1)

            dve.wait_ge(s_listT, 1)
            v.tensor_copy(row_i[:, :], bank[5][:, 0:NE]).then_inc(s_rows, 1)

            split13_low(At(0, 0))
            xeT_low(At(0, 0))

            def gate_weights_low():
                for b in range(2):
                    dve.wait_ge(w_att_hi, b + 1)
                    v.tensor_tensor(w_lo[:, b, 0:DC * D], raw[:, b, 0:DC * D],
                                    w_hi[:, b, 0:DC * D].bitcast(f32), ALU.subtract).then_inc(w_att_lo, 1)

            def phase_b(at):
                if at.next:
                    split13_low(at.next)
                if at.prev:
                    split2_low(at.prev)
                    heT_low(at.prev)
                if at.next:
                    xeT_low(at.next)
                if at.cur:
                    gate_expert(at.cur)
                else:
                    gate_weights_low()

            turns(dve, NE, phase_b, 3)

            v.memset(state[0:DK, 0, :], 0.0)
            dve.wait_ge(w_o_in, 16)
            w_o_raw = raw[:, 0, DC * D:2 * DC * D]
            for k in range(DC):
                scaled = v.tensor_scalar(w_o_raw[:, k * D:(k + 1) * D], w_o_raw[:, k * D:(k + 1) * D],
                                         gnorm[:, k:k + 1], None, ALU.mult)
            scaled.then_inc(w_o_scaled, 1)
            dve.wait_ge(w_o_scaled, 1)

            def decayed(t):
                def of(x):
                    return x[:, bass.ds(t.n(), 1), :].rearrange("p o k -> p (o k)")

                if t.past(1):
                    dve.wait_ge(c["gT_ps"], t.n())
                    dve.wait_ge(c["ds_ps"], t.n())
                v.tensor_tensor(q_mid, of(q_all), of(ex[:, 0, :, :]), ALU.mult)
                v.tensor_tensor(k_mid, of(k_all), of(exm), ALU.mult)
                v.tensor_copy(decay, ex[:, 3, bass.ds(t.n(), 1), :].to_broadcast([P, 2, DK]))
                v.tensor_tensor(qk_e, qk_all[:, :, bass.ds(t.n(), 1), :].rearrange("p a o k -> p a (o k)"),
                                ex[:, 1:3, bass.ds(t.n(), 1), :].rearrange("p a o k -> p a (o k)"), ALU.mult
                                ).then_inc(c["qk_e"], 1)
                dve.wait_ge(c["qk_e"], t.n(1))
                v.tensor_tensor(qk_c, qk_e.unsqueeze(2).to_broadcast([P, 2, 2, DK]),
                                chunk_of[:, :].unsqueeze(1).unsqueeze(3).to_broadcast([P, 2, 2, DK]), ALU.mult
                                ).then_inc(c["nat_done"], 1)

            def w_o_low():
                dve.wait_ge(w_att_hi, 3)
                v.tensor_tensor(w_lo[:, 0, DC * D:2 * DC * D], w_o_raw,
                                w_hi[:, 0, DC * D:2 * DC * D].bitcast(f32), ALU.subtract).then_inc(w_att_lo, 1)

            def mask_att(t):
                dve.wait_ge(c["at_ps"], t.n(1))
                if t.past(1):
                    dve.wait_ge(c["o_ps"], t.n())
                v.tensor_tensor(attT, bank[0][:, 0:P], causal[:, :], ALU.mult).then_inc(c["at_sb"], 1)

            def state_mid(t):
                dve.wait_ge(c["ds_ps"], t.n(1))
                dve.wait_ge(c["gT_sb"], t.n(1))
                if t.past(1):
                    dve.wait_ge(c["s_next"], t.n())
                v.scalar_tensor_tensor(state[DK:2 * DK, t.b, :], state[0:DK, t.b, :], att_l[0:DK, 3, 0:1],
                                       bank[1][0:DK, :], ALU.mult, ALU.add).then_inc(c["s_mid"], 1)

            def state_next(t):
                dve.wait_ge(c["s_mid"], t.n(1))
                v.scalar_tensor_tensor(state[0:DK, 1 - t.b, :], state[DK:2 * DK, t.b, :],
                                       att_l[DK:2 * DK, 3, DK:DK + 1], bank[1][DK:2 * DK, :],
                                       ALU.mult, ALU.add).then_inc(c["s_next"], 1)

            def o_out(t):
                dve.wait_ge(c["o_ps"], t.n(1))
                if t.past(1):
                    dve.wait_ge(c["oT_ps"], t.n())
                    dve.wait_ge(c["sq_done"], t.n())
                v.tensor_copy(o_sb, bank[2][:, :]).then_inc(c["o_sb"], 1)

            def gated(t):
                dve.wait_ge(c["rstd"], t.n(1))
                dve.wait_ge(c["sil_done"], t.n(1))
                if t.past(1):
                    dve.wait_ge(c["ogT_ps"], t.n())
                v.scalar_tensor_tensor(og, o_sb, orstd, sil, ALU.mult, ALU.mult).then_inc(c["og_done"], 1)

            def low_part(b, parts, high, done, t):
                dve.wait_ge(c[high], t.n(1))
                v.tensor_tensor(parts[1], split4(bank[b]), parts[0].bitcast(f32), ALU.subtract
                                ).then_inc(c[done], 1)

            def add_experts(t, some):
                for k in some:
                    before = (acc[:, bass.ds(t.n(), 1), :].rearrange("p o d -> p (o d)") if k == 0
                              else racc[:, t.b, :])
                    dve.wait_ge(gat_in[k], t.i * 32 + 16 * (t.off + 1))
                    if k:
                        dve.wait_ge(c["gat_used"], t.n() * TOPK + k)
                    v.scalar_tensor_tensor(racc[:, t.b, :], gat[:, k, :],
                                           gates[:, bass.ds(t.n(), 1), k:k + 1].rearrange("p o k -> p (o k)"),
                                           before, ALU.mult, ALU.add).then_inc(c["gat_used"], 1)

            def result(t):
                dve.wait_ge(c["out_ps"], t.n(1))
                dve.wait_ge(c["gat_used"], t.n(1) * TOPK)
                if t.past(2):
                    dve.wait_ge(res_out[t.b], t.i * 32 + 32 * (t.off // 2))
                v.tensor_tensor(res[:, t.b, :], racc[:, t.b, :], bank[7][:, :], ALU.add).then_inc(c["res_done"], 1)

            dve.wait_ge(g_decays, 1)
            decayed(At(0, 0))
            low_part(5, vT, "vT_hi", "vT_lo", At(0, 0))

            def phase_c(at):
                if at.cur:
                    mask_att(at.cur)
                    state_mid(at.cur)
                    state_next(at.cur)
                if at.next:
                    decayed(at.next)
                if at.prev:
                    low_part(3, ogT, "ogT_hi", "ogT_lo", at.prev)
                else:
                    w_o_low()
                if at.prev:
                    add_experts(at.prev, range(4, TOPK))
                if at.cur:
                    o_out(at.cur)
                if at.prev:
                    result(at.prev)
                if at.cur:
                    low_part(3, oT, "oT_hi", "oT_lo", at.cur)
                if at.next:
                    low_part(5, vT, "vT_hi", "vT_lo", at.next)
                if at.cur:
                    add_experts(at.cur, range(4))
                    gated(at.cur)

            turns(dve, NT, phase_c, 1)

        @block.scalar
        def _(act):
            s = nc.scalar

            def copy(out, in_):
                return s.activation(out, in_, ACT.Copy)

            act.wait_ge(s_c0, 48)
            copy(wr_hi[:, :, :], wrqk).then_inc(s_wr_hi, 1)
            act.wait_ge(s_wsh, 16)
            for k in range(2):
                part = slice(k * S13 // 2, (k + 1) * S13 // 2)
                copy(flat(w_hi)[:, part], flat(raw)[:, part]).then_inc(s_sh_hi, 1)
            for m in range(DC):
                act.wait_ge(s_wqT, m + 1)
                last = copy(wqT[:, m, :], bank[m][:, 0:256].bitcast(bf16))
            last.then_inc(s_wqe, 1)
            act.wait_ge(s_wqT, DC + 1)
            copy(wscale_bc[:, :], bank[4][:, :]).then_inc(s_wqe, 1)

            def xn2T_high(t):
                act.wait_ge(a["xn2T_ps"], t.n(1))
                if t.past(1):
                    act.wait_ge(a["wd_ps"], t.n())
                copy(xn2T[0], split4(bank[0])).then_inc(a["xn2T_hi"], 1)

            def xnT_out(t):
                act.wait_ge(a["xnT_ps"], t.n(1))
                if t.past(1):
                    act.wait_ge(a["s_ps"], t.n())
                copy(xnT, split4(bank[0])).then_inc(a["xnT_sb"], 1)

            def xqT_out(t):
                act.wait_ge(a["xqT_ps"], t.n(1))
                if t.past(1):
                    act.wait_ge(a["f_ps"], t.n())
                copy(xqT[:, :, :], bank[7][:, 0:256].bitcast(bf16).rearrange("p (c k) -> p c k", c=DC)
                     ).then_inc(a["xqT_sb"], 1)

            def router_exp(t):
                act.wait_ge(a["lg_ps"], t.n(1))
                if t.past(1):
                    act.wait_ge(a["gmax_done"], t.n())
                copy(qk_logits[:, bass.ds(t.n(), 1), :].rearrange("p o k -> p (o k)"),
                     bank[1][:, 256 + NE:256 + NE + 2 * DK])
                copy(glog[:, :], bank[1][:, 256:256 + NE]).then_inc(a["lg_sb"], 1)
                act.wait_ge(a["gmax_done"], t.n(1))
                if t.past(1):
                    act.wait_ge(a["mask_done"], t.n())
                s.activation(gexp[:, :], glog[:, :], ACT.Exp, bias=gmax[:, :], accum_out=gsum[:, :]
                             ).then_inc(a["gexp_done"], 1)

            def att_exp(t):
                act.wait_ge(a["dist_done"], t.n(1))
                if t.past(1):
                    act.wait_ge(a["eT_ps1"], t.n())
                    act.wait_ge(a["esum_done"], t.n())
                s.activation(probs[0:SEGQ, :, 0:SEGQ], dist[0:SEGQ, :, :], ACT.Exp, scale=ATT_SCALE)
                s.activation(probs[SEGQ:P, :, SEGQ:P], dist[SEGQ:P, :, :], ACT.Exp, scale=ATT_SCALE
                             ).then_inc(a["exp_done"], 1)

            def silu_half(t, half):
                act.wait_ge(a["wa_ps" if half == 0 else "wc_ps"], t.n(1))
                if half == 0 and t.past(1):
                    act.wait_ge(a["hT_ps"], t.n())
                s.activation(hs[:, half * SQ:(half + 1) * SQ], bank[6][:, 0:SQ], ACT.Silu
                             ).then_inc(a["silA" if half == 0 else "silB"], 1)

            def eT_out(t):
                if t.past(1):
                    act.wait_ge(a["att_ps"], t.n())
                act.wait_ge(a["eT_ps0"], t.n(1))
                copy(eT[:, 0:4, :], split4(bank[4]))
                act.wait_ge(a["eT_ps1"], t.n(1))
                copy(eT[:, 4:8, :], split4(bank[5])).then_inc(a["eT_sb"], 1)

            def hsT_high(t):
                act.wait_ge(a["hT_ps"], t.n(1))
                if t.past(1):
                    act.wait_ge(a["z_ps"], t.n())
                copy(hsT[0][:, 0:4, :], split4(bank[4]))
                copy(hsT[0][:, 4, :], bank[5][:, 0:P])
                copy(hsT[0][0:SR, 5, :], bank[5][0:SR, P:2 * P]).then_inc(a["hT_hi"], 1)

            def phase_a(at):
                if at.prev:
                    xn2T_high(at.prev)
                if at.cur:
                    att_exp(at.cur)
                if at.prev:
                    router_exp(at.prev)
                    silu_half(at.prev, 0)
                if at.cur:
                    eT_out(at.cur)
                if at.prev:
                    silu_half(at.prev, 1)
                if at.prev:
                    hsT_high(at.prev)
                if at.next:
                    xnT_out(at.next)
                    xqT_out(at.next)

            act.wait_ge(s_zero, 6)
            xnT_out(At(0, 0))
            xqT_out(At(0, 0))
            act.wait_ge(s_wsh2, 32)
            copy(flat(w_hi)[:, S13:S13 + S2 - D], flat(raw)[:, S13:S13 + S2 - D])
            copy(flat(w_hi)[0:SR, S13 + S2 - D:S13 + S2], flat(raw)[0:SR, S13 + S2 - D:S13 + S2]
                 ).then_inc(s_sh_hi, 1)
            turns(act, NT, phase_a, 1)

            def gates_exp():
                act.wait_ge(g_steps, 2)
                s.activation(k_exp, k_log, ACT.Exp, scale=-1.0)
                s.activation(q_dist, q_dist, ACT.Exp).then_inc(g_exp, 1)
                act.wait_ge(g_steps, 5)
                s.activation(k_gate, k_all, ACT.Exp).then_inc(g_exp, 1)
                act.wait_ge(g_exp, 2)
                s.activation(gfn, k_gate, ACT.Ln, bias=1.0).then_inc(g_ln, 1)
                act.wait_ge(g_cum, 1)
                act.wait_ge(g_steps, 7)
                for m in range(4):
                    s.activation(ex[:, m, :, :], cum_ps[m].rearrange("p (t k) -> p t k", t=NT), ACT.Exp, scale=-1.0)
                s.activation(exm, cum_ps[0].rearrange("p (t k) -> p t k", t=NT), ACT.Exp).then_inc(g_decays, 1)

            def split13_high(e):
                act.wait_ge(w13_in[e.b], e.dma())
                if e.past(2):
                    act.wait_ge(e_["h3_ps"], e.n(-1))
                copy(w_hi[:, e.b, 0:W13], raw[:, e.b, 0:W13]).then_inc(e_["w13_hi"], 1)

            def split2_high(e):
                act.wait_ge(w2_in[e.b], e.dma2())
                if e.past(2):
                    act.wait_ge(e_["y_ps"], e.n(-1))
                copy(w_hi[:, e.b, W13:WE - D], raw[:, e.b, W13:WE - D])
                copy(w_hi[0:IB, e.b, WE - D:WE], raw[0:IB, e.b, WE - D:WE]).then_inc(e_["w2_hi"], 1)

            act.wait_ge(a["z_ps"], NT)
            split13_high(At(0, 0))
            act.wait_ge(a["acc_done"], NT)
            gates_exp()

            def gate_weights_high():
                act.wait_ge(w_gate_in, 16)
                copy(w_hi[:, 0, 0:DC * D], raw[:, 0, 0:DC * D]).then_inc(w_att_hi, 1)
                act.wait_ge(w_gate_in2, 16)
                copy(w_hi[:, 1, 0:DC * D], raw[:, 1, 0:DC * D]).then_inc(w_att_hi, 1)

            def silu_expert(e):
                act.wait_ge(e_["h1_ps"], e.n(1))
                if e.past(1):
                    act.wait_ge(e_["h_done"], e.n())
                s.activation(hsil, bank[0][:, 0:IE], ACT.Silu).then_inc(e_["sil_done"], 1)

            def heT_high(e):
                act.wait_ge(e_["hT_ps"], e.n(1))
                if e.past(1):
                    act.wait_ge(e_["y_ps"], e.n())
                copy(heT[0][:, 0:2, :], bank[3][:, 0:2 * P].rearrange("p (c k) -> p c k", c=2))
                copy(heT[0][0:IB, 2, :], bank[3][0:IB, 2 * P:3 * P]).then_inc(e_["hT_hi"], 1)

            def xeT_high(e):
                act.wait_ge(e_["xeT_ps"], e.n(1))
                if e.past(2):
                    act.wait_ge(e_["h3_ps"], e.n(-1))
                copy(xeT[e.b][0], split4(bank[2])).then_inc(e_["xeT_hi"], 1)

            def ye_sb(e):
                act.wait_ge(e_["y_ps"], e.n(1))
                if e.past(2):
                    act.wait_ge(ye_out[e.b], e.dma(1))
                copy(ye[:, e.b, :], bank[4][:, :]).then_inc(e_["y_sb"], 1)

            xeT_high(At(0, 0))
            split13_high(At(0, 1))

            def phase_b(at):
                if at.cur:
                    silu_expert(at.cur)
                if at.prev:
                    heT_high(at.prev)
                if at.next:
                    xeT_high(at.next)
                if at.after:
                    split13_high(at.after)
                if not at.cur:
                    gate_weights_high()
                if at.prev:
                    ye_sb(at.prev)
                if at.cur:
                    split2_high(at.cur)

            turns(act, NE, phase_b, 3)

            def square(t):
                act.wait_ge(c["o_sb"], t.n(1))
                if t.past(1):
                    act.wait_ge(c["og_done"], t.n())
                s.activation(sil, o_sb, ACT.Square, accum_out=osq).then_inc(c["sq_done"], 1)

            def high_part(b, parts, ready, used_by, done, t):
                act.wait_ge(c[ready], t.n(1))
                if t.past(1):
                    act.wait_ge(c[used_by], t.n())
                copy(parts[0], split4(bank[b])).then_inc(c[done], 1)

            def gT_out(t):
                act.wait_ge(c["gT_ps"], t.n(1))
                if t.past(1):
                    act.wait_ge(c["o_ps"], t.n())
                    act.wait_ge(c["s_next"], t.n())
                copy(att_l[0:DK, 0:2, :], split4(bank[6])[0:DK, 0:2, :])
                copy(att_l[0:2 * DK, 2:4, :], split4(bank[6])[0:2 * DK, 2:4, :]).then_inc(c["gT_sb"], 1)

            def silu_gate(t):
                act.wait_ge(c["go_ps"], t.n(1))
                act.wait_ge(c["sq_done"], t.n(1))
                s.activation(sil, bank[4][:, :], ACT.Silu).then_inc(c["sil_done"], 1)

            gT_out(At(0, 0))
            high_part(5, vT, "vT_ps", "wig_ps", "vT_hi", At(0, 0))
            act.wait_ge(w_o_scaled, 1)
            act.wait_ge(e_["y_ps"], NE)
            copy(w_hi[:, 0, DC * D:2 * DC * D], raw[:, 0, DC * D:2 * DC * D]).then_inc(w_att_hi, 1)

            def phase_c(at):
                if at.prev:
                    high_part(3, ogT, "ogT_ps", "out_ps", "ogT_hi", at.prev)
                if at.cur:
                    square(at.cur)
                    high_part(3, oT, "oT_ps", "go_ps", "oT_hi", at.cur)
                if at.next:
                    gT_out(at.next)
                if at.next:
                    high_part(5, vT, "vT_ps", "wig_ps", "vT_hi", at.next)
                if at.cur:
                    silu_gate(at.cur)

            turns(act, NT, phase_c, 1)

        @block.tensor
        def _(pe):
            te = nc.tensor

            def chunks(out, lhsT, rhs, n, first=True, last=True):
                for k in range(n):
                    ins = te.matmul(out, lhsT(k), rhs(k), start=first and k == 0, stop=last and k == n - 1)
                return ins

            def product(out, lhs, rhs, k, left, right, n, rows, start, stop):
                w = P if rows is None or k < n - 1 else rows
                return te.matmul(out, lhs[left][0:w, k, :], rhs(right, w, k), start=start, stop=stop)

            def high_chunks(out, lhs, rhs, n, rows=None, first=True):
                for k in range(n):
                    product(out, lhs, rhs, k, 0, 0, n, rows, first and k == 0, False)
                    product(out, lhs, rhs, k, 0, 1, n, rows, False, False)

            def low_chunks(out, lhs, rhs, n, rows=None, last=True):
                for k in range(n):
                    ins = product(out, lhs, rhs, k, 1, 0, n, rows, False, last and k == n - 1)
                return ins

            def split_chunks(out, lhs, low_ready, value, rhs, n, rows=None, first=True, last=True):
                high_chunks(out, lhs, rhs, n, rows, first)
                pe.wait_ge(low_ready, value)
                return low_chunks(out, lhs, rhs, n, rows, last)

            def transposes(b, src, n=DC):
                for k in range(n):
                    ins = te.transpose(bank[b][:, k * P:(k + 1) * P], src[:, k * P:(k + 1) * P], ident[:, :])
                return ins

            pe.wait_ge(s_set, 1)
            pe.wait_ge(s_zero, 6)
            pe.wait_ge(s_wq, 2 * DC)
            for m in range(DC):
                o = bank[m][:, 0:256].bitcast(bf16)
                for k in range(DC):
                    ins = te.transpose(o[:, k * P:(k + 1) * P], wq[:, k, m * P:(m + 1) * P], ident_bf[:, :])
                ins.then_inc(s_wqT, 1)
            te.matmul(bank[4][:, :], ones_mat[:, :], wdiag.rearrange("p c k -> p (c k)"), start=True, stop=True
                      ).then_inc(s_wqT, 1)
            pe.wait_ge(s_wqe, 2)
            pe.wait_ge(s_c0, 48)
            pe.wait_ge(s_const, 1)

            xqT_ps = bank[7][:, 0:256].bitcast(bf16)
            lg_ps = bank[1][:, 256:256 + P]
            pos_ps = bank[1][:, 384:384 + NE]

            def xn2_T(t, with_cur):
                pe.wait_ge(a["xn2_done"], t.n(1))
                pe.wait_ge(a["xnT_sb"], t.n(2) if with_cur else t.n(1))
                transposes(0, xn2[:, t.b, :]).then_inc(a["xn2T_ps"], 1)

            def xn_T(t):
                pe.wait_ge(a["xn_done"], t.n(1))
                if t.past(2):
                    pe.wait_ge(a["xn2T_lo"], t.n(-1))
                elif t.past(1):
                    pe.wait_ge(a["xnT_sb"], 1)
                transposes(0, xn[:, t.b, :]).then_inc(a["xnT_ps"], 1)

            def xq_T(t):
                pe.wait_ge(a["xq_done"], t.n(1))
                if t.past(2):
                    pe.wait_ge(a["hB_done"], t.n(-1))
                elif t.past(1):
                    pe.wait_ge(a["xqT_sb"], 1)
                for k in range(DC):
                    ins = te.transpose(xqT_ps[:, k * P:(k + 1) * P], xq[:, k * P:(k + 1) * P], ident_bf[:, :])
                ins.then_inc(a["xqT_ps"], 1)

            def router_weights(part, w, k):
                return (wr_hi, wr_lo)[part][:, k, :]

            def shared_weights(quarter):
                return lambda part, w, k: sh13[part][:, k, quarter * SQ:(quarter + 1) * SQ]

            def logits_and_shared(t):
                if t.past(1):
                    pe.wait_ge(a["slot_steps"], t.n() * 7)
                high_chunks(lg_ps, xn2T, router_weights, DC)
                if t.past(1):
                    pe.wait_ge(a["acc_done"], t.n())
                else:
                    pe.wait_ge(s_sh_lo, 2)
                high_chunks(bank[6][:, 0:SQ], xn2T, shared_weights(0), DC)
                pe.wait_ge(a["xn2T_lo"], t.n(1))
                low_chunks(lg_ps, xn2T, router_weights, DC).then_inc(a["lg_ps"], 1)
                low_chunks(bank[6][:, 0:SQ], xn2T, shared_weights(0), DC).then_inc(a["wa_ps"], 1)

            def shared(t, b, part, done):
                split_chunks(bank[b][:, 0:SQ], xn2T, a["xn2T_lo"], t.n(1),
                             shared_weights(part), DC).then_inc(a[done], 1)

            def att_scores(t):
                pe.wait_ge(a["xnT_sb"], t.n(1))
                pe.wait_ge(a["xnh_done"], t.n(1))
                if t.past(1):
                    pe.wait_ge(a["x1_done"], t.n())
                for k in range(DC):
                    for r in range(2):
                        ins = te.matmul(bank[2][r * SEGQ:(r + 1) * SEGQ, k * P:(k + 1) * P],
                                        xnT[:, k, r * SEGQ:(r + 1) * SEGQ],
                                        xn_heads[:, 2 * k + r, :, :].rearrange("p h j -> p (h j)"),
                                        start=True, stop=True)
                ins.then_inc(a["s_ps"], 1)

            def quantised(t):
                pe.wait_ge(a["xqT_sb"], t.n(1))
                if t.past(1):
                    pe.wait_ge(a["y_scaled"], t.n())
                chunks(bank[3][:, :], lambda k: xqT[:, k, :], lambda k: wqT[:, k, :], DC).then_inc(a["f_ps"], 1)

            def positions(t):
                pe.wait_ge(a["mask_done"], t.n(1))
                pe.wait_ge(a["lg_sb"], t.n(1))
                if t.past(1):
                    pe.wait_ge(a["slot_steps"], t.n() * 7)
                te.matmul(pos_ps, before_bf[:, :], mask_bf[:, :], start=True, stop=False)
                te.matmul(pos_ps, ones_bf[:, :], msum_bf[:, :], start=False, stop=True).then_inc(a["pos_ps"], 1)

            def probs_T(t):
                pe.wait_ge(a["exp_done"], t.n(1))
                if t.past(2):
                    pe.wait_ge(a["hT_lo"], t.n(-1))
                for half in range(2):
                    for k in range(4):
                        ins = te.transpose(bank[4 + half][:, k * P:(k + 1) * P], probs[:, 4 * half + k, :],
                                           ident[:, :])
                    ins.then_inc(a[f"eT_ps{half}"], 1)

            def attention(t):
                pe.wait_ge(a["eT_sb"], t.n(1))
                pe.wait_ge(a["dist_done"], t.n(1))
                for k in range(HP):
                    ins = te.matmul(bank[2][:, k * 2 * HD:(k + 1) * 2 * HD], eT[:, k, :],
                                    xn[:, t.b, k * 2 * HD:(k + 1) * 2 * HD], start=True, stop=True)
                ins.then_inc(a["att_ps"], 1)

            def h_T(t, with_cur):
                pe.wait_ge(a["hB_done"], t.n(1))
                pe.wait_ge(a["hA_done"], t.n(1))
                pe.wait_ge(a["eT_sb"], t.n(2) if with_cur else t.n(1))
                for k in range(SC):
                    w = P if k < SC - 1 else SR
                    ins = te.transpose(bank[4 + k // 4][0:w, (k % 4) * P:(k % 4 + 1) * P],
                                       hs[:, k * P:k * P + w], ident[:, :])
                ins.then_inc(a["hT_ps"], 1)

            def shared_out(t):
                pe.wait_ge(a["hT_hi"], t.n(1))
                pe.wait_ge(a["silB"], t.n(1))
                split_chunks(bank[6][:, :], hsT, a["hT_lo"], t.n(1),
                             lambda half, w, k: sh2[half][0:w, k, :], SC, SR).then_inc(a["z_ps"], 1)

            def phase_a(at):
                t, p = at.cur, at.prev
                if t:
                    att_scores(t)
                if p:
                    xn2_T(p, t is not None)
                if t:
                    quantised(t)
                if p:
                    if not p.past(1):
                        pe.wait_ge(s_wr_lo, 1)
                    pe.wait_ge(a["xn2T_hi"], p.n(1))
                    logits_and_shared(p)
                    pe.wait_ge(a["xqT_sb"], p.n(2) if t else p.n(1))
                    shared(p, 7, 2, "wb_ps")
                if t:
                    probs_T(t)
                if p:
                    pe.wait_ge(a["silA"], p.n(1))
                    shared(p, 6, 1, "wc_ps")
                    pe.wait_ge(a["hA_done"], p.n(1))
                    shared(p, 7, 3, "wd_ps")
                if t:
                    attention(t)
                else:
                    positions(p)
                if p:
                    h_T(p, t is not None)
                if at.next:
                    xn_T(at.next)
                    xq_T(at.next)
                if t and p:
                    positions(p)
                if p:
                    shared_out(p)

            xn_T(At(0, 0))
            xq_T(At(0, 0))
            turns(pe, NT, phase_a, 1)

            pe.wait_ge(a["acc_done"], NT)
            pe.wait_ge(a["slot_steps"], 7 * NT)

            def xe_T(e):
                pe.wait_ge(xe_in[e.b], e.dma())
                if e.past(1):
                    pe.wait_ge(e_["xeT_lo"], e.n())
                transposes(2, xe[:, e.b, :]).then_inc(e_["xeT_ps"], 1)

            def first(e):
                pe.wait_ge(e_["xeT_hi"], e.n(1))
                pe.wait_ge(e_["w13_lo"], e.n(1))
                if e.past(1):
                    pe.wait_ge(e_["sil_done"], e.n())
                split_chunks(bank[0][:, 0:IE], xeT[e.b], e_["xeT_lo"], e.n(1),
                             lambda part, w, k: e13[part][:, e.b, k, 0:IE], DC).then_inc(e_["h1_ps"], 1)
                if e.past(1):
                    pe.wait_ge(e_["h_done"], e.n())
                split_chunks(bank[1][:, 0:IE], xeT[e.b], e_["xeT_lo"], e.n(1),
                             lambda part, w, k: e13[part][:, e.b, k, IE:I2], DC).then_inc(e_["h3_ps"], 1)

            def he_T(e):
                pe.wait_ge(e_["h_done"], e.n(1))
                if not e.past(1):
                    pe.wait_ge(g_decays, 1)
                else:
                    pe.wait_ge(e_["hT_lo"], e.n())
                for k in range(3):
                    w = P if k < 2 else IB
                    ins = te.transpose(bank[3][0:w, k * P:(k + 1) * P], he[:, e.b, k * P:k * P + w], ident[:, :])
                ins.then_inc(e_["hT_ps"], 1)

            def second(e):
                pe.wait_ge(e_["hT_hi"], e.n(1))
                pe.wait_ge(e_["w2_lo"], e.n(1))
                pe.wait_ge(e_["w2_lo2"], e.n(1))
                if e.past(1):
                    pe.wait_ge(e_["y_sb"], e.n())
                split_chunks(bank[4][:, :], heT, e_["hT_lo"], e.n(1),
                             lambda part, w, k: e2[part][0:w, e.b, k, :], 3, IB).then_inc(e_["y_ps"], 1)

            pe.wait_ge(s_lists, 32)
            te.transpose(bank[5][:, 0:NE], lists[0:NE, :], ident[0:NE, 0:NE]).then_inc(s_listT, 1)
            pe.wait_ge(g_ln, 1)
            for k, m in enumerate((from_mid, causal, to_last, same_chunk)):
                ins = te.matmul(cum_ps[k], m[:, :], gfn.rearrange("p t k -> p (t k)"), start=True, stop=True)
            ins.then_inc(g_cum, 1)
            xe_T(At(0, 0))

            def phase_b(at):
                if at.cur:
                    first(at.cur)
                if at.prev:
                    he_T(at.prev)
                if at.next:
                    xe_T(at.next)
                if at.prev:
                    second(at.prev)

            turns(pe, NE, phase_b, 3)

            pe.wait_ge(e_["y_sb"], NE)

            def attT_ps(t):
                pe.wait_ge(c["gT_sb"], t.n(1))
                if t.past(1):
                    pe.wait_ge(c["at_sb"], t.n())
                te.matmul(bank[0][:, 0:P], att_l[0:DK, 1, :], att_l[0:DK, 0, :], start=True, stop=True
                          ).then_inc(c["at_ps"], 1)

            def state_add(t):
                pe.wait_ge(v_in[t.b], t.dma())
                pe.wait_ge(c["nat_done"], t.n(1))
                if t.past(1):
                    pe.wait_ge(c["s_next"], t.n())
                te.matmul(bank[1][0:2 * DK, :], qk_c[:, 1, :, :].rearrange("p c k -> p (c k)"), v_t[:, t.b, :],
                          start=True, stop=True).then_inc(c["ds_ps"], 1)

            def gate_in(t):
                pe.wait_ge(c["vT_hi"], t.n(1))
                if not t.past(1):
                    pe.wait_ge(w_att_lo, 2)
                if t.past(1):
                    pe.wait_ge(c["sil_done"], t.n())
                split_chunks(bank[4][:, :], vT, c["vT_lo"], t.n(1), lambda part, w, k: w_ig2[part][:, k, :], DC,
                             last=False).then_inc(c["wig_ps"], 1)

            def gate_o(t):
                pe.wait_ge(c["oT_hi"], t.n(1))
                split_chunks(bank[4][:, :], oT, c["oT_lo"], t.n(1), lambda part, w, k: w_og2[part][:, k, :], DC,
                             first=False).then_inc(c["go_ps"], 1)

            def output(t):
                pe.wait_ge(c["at_sb"], t.n(1))
                pe.wait_ge(c["s_mid"], t.n(1))
                if t.past(1):
                    pe.wait_ge(c["o_sb"], t.n())
                te.matmul(bank[2][:, :], attT, v_t[:, t.b, :], start=True, stop=False)
                te.matmul(bank[2][:, :], att_l[0:2 * DK, 2, :], state[0:2 * DK, t.b, :], start=False, stop=True
                          ).then_inc(c["o_ps"], 1)

            def o_T(t):
                pe.wait_ge(c["o_sb"], t.n(1))
                if t.past(1):
                    pe.wait_ge(c["ogT_lo"], t.n())
                transposes(3, o_sb).then_inc(c["oT_ps"], 1)

            def og_T(t):
                pe.wait_ge(c["og_done"], t.n(1))
                pe.wait_ge(c["oT_lo"], t.n(1))
                transposes(3, og).then_inc(c["ogT_ps"], 1)

            def out_product(t):
                pe.wait_ge(c["ogT_hi"], t.n(1))
                if not t.past(1):
                    pe.wait_ge(w_att_lo, 3)
                if t.past(1):
                    pe.wait_ge(c["res_done"], t.n())
                split_chunks(bank[7][:, :], ogT, c["ogT_lo"], t.n(1), lambda part, w, k: w_o2[part][:, k, :], DC
                             ).then_inc(c["out_ps"], 1)

            def decayed_T(t):
                pe.wait_ge(c["nat_done"], t.n(1))
                if t.past(1):
                    pe.wait_ge(c["gT_sb"], t.n())
                te.transpose(bank[6][0:DK, 0:P], q_mid, ident[:, :])
                te.transpose(bank[6][0:DK, P:2 * P], k_mid, ident[:, :])
                te.transpose(bank[6][0:2 * DK, 2 * P:3 * P], qk_c[:, 0, :, :].rearrange("p c k -> p (c k)"),
                             ident[:, :])
                te.transpose(bank[6][0:2 * DK, 3 * P:4 * P], decay.rearrange("p c k -> p (c k)"), ident[:, :]
                             ).then_inc(c["gT_ps"], 1)

            def v_T(t):
                pe.wait_ge(v_in[t.b], t.dma())
                if t.past(1):
                    pe.wait_ge(c["vT_lo"], t.n())
                transposes(5, v_t[:, t.b, :]).then_inc(c["vT_ps"], 1)

            decayed_T(At(0, 0))
            v_T(At(0, 0))

            def phase_c(at):
                if at.cur:
                    attT_ps(at.cur)
                    state_add(at.cur)
                    gate_in(at.cur)
                if at.prev:
                    og_T(at.prev)
                if at.cur:
                    output(at.cur)
                if at.prev:
                    out_product(at.prev)
                if at.cur:
                    o_T(at.cur)
                if at.next:
                    decayed_T(at.next)
                if at.next:
                    v_T(at.next)
                if at.cur:
                    gate_o(at.cur)

            turns(pe, NT, phase_c, 1)


def kernel(**inputs):
    import numpy as np
    import concourse.bacc as bacc
    from concourse.bass_utils import run_bass_kernel_spmd

    P = 128

    def rows_first(w):
        return np.ascontiguousarray(w.reshape(-1, P, w.shape[-1]).transpose(1, 0, 2))

    g = {k: np.asarray(a) for k, a in inputs.items()}
    x = g["L0_attn_x"]
    w13 = np.concatenate([g["L1_ffn_w1"], g["L1_ffn_w3"]], 1)
    w13 = w13.transpose(0, 2, 1).reshape(w13.shape[0], -1, P, w13.shape[1]).transpose(0, 2, 1, 3)
    w2 = g["L1_ffn_w2"].transpose(0, 2, 1)
    w2a = w2[:, :2 * P].reshape(w2.shape[0], 2, P, -1).transpose(0, 2, 1, 3)
    arrays = {
        "x": x.reshape(x.shape[1:]),
        "w_ffn": g["L0_ffn_weight"],
        "b_ffn": g["L0_ffn_bias"],
        "w_rqk": rows_first(np.concatenate([g["L1_ffn_gate_w"], g["L1_attn_Wq"], g["L1_attn_Wk"]], 0).T),
        "w_og": rows_first(g["L1_attn_Wog"].T),
        "w_ig": rows_first(g["L1_attn_Wig"].T),
        "w_o": rows_first(g["L1_attn_Wo"].T),
        "g_norm": g["L1_attn_g_norm_w"].reshape(-1, P).T,
        "w_sh13": rows_first(np.concatenate([g["L1_ffn_sw1"], g["L1_ffn_sw3"]], 0).T),
        "w_sh2": g["L1_ffn_sw2"].T,
        "w13": w13,
        "w2a": w2a,
        "w2b": w2[:, 2 * P:],
    }
    arrays = {k: np.ascontiguousarray(v) for k, v in arrays.items()}
    nc = bacc.Bacc("TRN2", target_bir_lowering=False, num_devices=1)
    f32 = mybir.dt.float32
    args = [nc.dram_tensor("in_" + k, v.shape, f32, kind="ExternalInput").ap() for k, v in arrays.items()]
    out = nc.dram_tensor("out", arrays["x"].shape, f32, kind="ExternalOutput").ap()
    xn_rows = nc.dram_tensor("xn_rows", arrays["x"].shape, f32, kind="Internal").ap()
    ye_rows = nc.dram_tensor("ye_rows", (w13.shape[0] * P, x.shape[2]), f32, kind="Internal").ap()
    slot_token = nc.dram_tensor("slot_token", (w13.shape[0] * P + 6 * x.shape[1], 1), f32, kind="Internal").ap()
    two_layers(nc, *args, out, xn_rows, ye_rows, slot_token)
    r = run_bass_kernel_spmd(nc, [{"in_" + k: v for k, v in arrays.items()}], core_ids=[0])
    return r.results[0]["out"].reshape(x.shape)
```
